# Optimizing a Trainium2 kernel written in Bass

```python
import numpy as np
import jax
import jax.numpy as jnp

def _softmax(x, axis=-1):
    return jax.nn.softmax(x, axis=axis)

def _gelu(x):
    return jax.nn.gelu(x, approximate=True)

def _silu(x):
    return jax.nn.silu(x)

def _sigmoid(x):
    return jax.nn.sigmoid(x)

def _layernorm(x, axis=-1, eps=1e-05):
    m = jnp.mean(x, axis=axis, keepdims=True)
    v = jnp.var(x, axis=axis, keepdims=True)
    return (x - m) / jnp.sqrt(v + eps)

def _scatter_add(tgt, idx, src, axis=0):
    return tgt.at[idx].add(src)

def _segment_sum(src, seg, n):
    return jax.ops.segment_sum(src, seg, n)
kernel_name = 'mk_gnn_ffn_d1_gnn_r8_961ee9'

def setup_inputs(seed: int=0):
    np.random.seed(seed)
    _w = jnp.asarray

    def _rec_inputs():
        import jax
        import jax.numpy as jnp
        _gk = jax.random.key(seed)
        x = -0.0001126 + 1 * jax.random.normal(jax.random.fold_in(_gk, 1), (6250, 768), jnp.float32)
        src = jax.random.randint(jax.random.fold_in(_gk, 2), (100000,), 0, 6250, jnp.int32)
        dst = jnp.minimum((6250 * jax.random.uniform(jax.random.fold_in(_gk, 3), (100000,)) ** 2.0).astype(jnp.int32), 49999)
        _o = jnp.argsort(dst, stable=True)
        src = src[_o]
        dst = dst[_o]
        return (x, src, dst)
    x, src, dst = _rec_inputs()

    def _L0_gnn_setup():
        import jax, jax.numpy as jnp
        import numpy as np
        N_NODES = 1250
        D = 768
        N_EDGES = 20000

        def gcn_conv(x, W, b, src, dst, n_nodes):
            h = x @ W
            deg = jax.ops.segment_sum(jnp.ones_like(dst, dtype=h.dtype), dst, num_segments=n_nodes)
            dinv = jnp.where(deg > 0, jax.lax.rsqrt(deg), 0.0)
            norm = dinv[src] * dinv[dst]
            msgs = h[src] * norm[:, None]
            out = jax.ops.segment_sum(msgs, dst, num_segments=n_nodes)
            return out + b

        def add_self_loops(edge_index, n_nodes):
            loop = jnp.arange(n_nodes, dtype=edge_index.dtype)
            src = jnp.concatenate([edge_index[0], loop])
            dst = jnp.concatenate([edge_index[1], loop])
            return (src, dst)
        key = jax.random.key(seed)
        k1, k2, k3, k4 = jax.random.split(key, 4)
        x = jax.random.normal(k1, (N_NODES, D), dtype=jnp.float32)
        edge_index = jax.random.randint(k2, (2, N_EDGES), 0, N_NODES, dtype=jnp.int32)
        glorot = float(np.sqrt(6.0 / (D + D)))
        W1 = jax.random.uniform(k3, (D, D), jnp.float32, -glorot, glorot)
        W2 = jax.random.uniform(k4, (D, D), jnp.float32, -glorot, glorot)
        b1 = jnp.zeros((D,), jnp.float32)
        b2 = jnp.zeros((D,), jnp.float32)
        return {'x': x, 'W1': W1, 'b1': b1, 'W2': W2, 'b2': b2, 'edge_index': edge_index}
    _L0_gnn_all = _L0_gnn_setup()
    _L0_gnn_in = {k: v for k, v in _L0_gnn_all.items() if k in ('W1', 'b1', 'W2', 'b2')}
    del _L0_gnn_all

    def _L0_ffn_setup():
        import jax, jax.numpy as jnp
        import numpy as np
        B, L, D = (4, 1024, 768)
        E, S, H = (32, 32, 384)
        EPS = 1e-12

        def _l2norm(v, axis):
            n = jnp.sqrt(jnp.sum(v * v, axis=axis, keepdims=True))
            return v / jnp.maximum(n, EPS)
        key = jax.random.key(seed)
        ks = jax.random.split(key, 6)
        x = jax.random.normal(ks[0], (B, L, D), dtype=jnp.float32)
        phi = jax.random.normal(ks[1], (D, E, S), dtype=jnp.float32) / np.sqrt(D)
        scale = jnp.ones((1,), dtype=jnp.float32)
        w1 = jax.random.normal(ks[2], (E, D, H), dtype=jnp.float32) / np.sqrt(D)
        b1 = jax.random.normal(ks[3], (E, H), dtype=jnp.float32) * 0.01
        w2 = jax.random.normal(ks[4], (E, H, D), dtype=jnp.float32) / np.sqrt(H)
        b2 = jax.random.normal(ks[5], (E, D), dtype=jnp.float32) * 0.01
        return {'x': x, 'phi': phi, 'scale': scale, 'w1': w1, 'b1': b1, 'w2': w2, 'b2': b2}
    _L0_ffn_all = _L0_ffn_setup()
    _L0_ffn_in = {k: v for k, v in _L0_ffn_all.items() if k in ('phi', 'scale', 'w1', 'b1', 'w2', 'b2')}
    del _L0_ffn_all
    return {'x': x, 'src': src, 'dst': dst, 'L0_gnn_W1': _L0_gnn_in['W1'], 'L0_gnn_b1': _L0_gnn_in['b1'], 'L0_gnn_W2': _L0_gnn_in['W2'], 'L0_gnn_b2': _L0_gnn_in['b2'], 'L0_ffn_phi': _L0_ffn_in['phi'], 'L0_ffn_scale': _L0_ffn_in['scale'], 'L0_ffn_w1': _L0_ffn_in['w1'], 'L0_ffn_b1': _L0_ffn_in['b1'], 'L0_ffn_w2': _L0_ffn_in['w2'], 'L0_ffn_b2': _L0_ffn_in['b2']}

def reference(x, src, dst, L0_gnn_W1, L0_gnn_b1, L0_gnn_W2, L0_gnn_b2, L0_ffn_phi, L0_ffn_scale, L0_ffn_w1, L0_ffn_b1, L0_ffn_w2, L0_ffn_b2):
    import jax
    import jax.numpy as jnp

    def _L0_gnn_ref(x, W1, b1, W2, b2, edge_index):
        import jax, jax.numpy as jnp
        import numpy as np
        N_NODES = 1250
        D = 768
        N_EDGES = 20000

        def gcn_conv(x, W, b, src, dst, n_nodes):
            h = x @ W
            deg = jax.ops.segment_sum(jnp.ones_like(dst, dtype=h.dtype), dst, num_segments=n_nodes)
            dinv = jnp.where(deg > 0, jax.lax.rsqrt(deg), 0.0)
            norm = dinv[src] * dinv[dst]
            msgs = h[src] * norm[:, None]
            out = jax.ops.segment_sum(msgs, dst, num_segments=n_nodes)
            return out + b

        def add_self_loops(edge_index, n_nodes):
            loop = jnp.arange(n_nodes, dtype=edge_index.dtype)
            src = jnp.concatenate([edge_index[0], loop])
            dst = jnp.concatenate([edge_index[1], loop])
            return (src, dst)
        n = x.shape[0]
        src, dst = add_self_loops(edge_index, n)
        h = gcn_conv(x, W1, b1, src, dst, n)
        h = jax.nn.relu(h)
        out = gcn_conv(h, W2, b2, src, dst, n)
        return out

    def _L0_ffn_ref(x, phi, scale, w1, b1, w2, b2):
        import jax, jax.numpy as jnp
        import numpy as np
        B, L, D = (4, 1024, 768)
        E, S, H = (32, 32, 384)
        EPS = 1e-12

        def _l2norm(v, axis):
            n = jnp.sqrt(jnp.sum(v * v, axis=axis, keepdims=True))
            return v / jnp.maximum(n, EPS)
        b, l, d = x.shape
        xn = _l2norm(x, axis=2)
        phin = scale * _l2norm(phi, axis=0)
        logits = jnp.einsum('bld,des->bles', xn, phin)
        d_w = jax.nn.softmax(logits, axis=-1)
        c_w = jax.nn.softmax(logits.reshape(b, l, E * S), axis=-1)
        slots = jnp.einsum('bld,bles->besd', xn, d_w)
        h = jax.nn.gelu(jnp.einsum('besd,edh->besh', slots, w1) + b1[:, None, :], approximate=False)
        eo = jnp.einsum('besh,ehd->besd', h, w2) + b2[:, None, :]
        eo = eo.reshape(b, E * S, d)
        return jnp.einsum('bkd,blk->bld', eo, c_w)
    edge_index = jnp.stack([src, dst])
    x = x + _L0_gnn_ref(_layernorm(x, axis=-1), L0_gnn_W1, L0_gnn_b1, L0_gnn_W2, L0_gnn_b2, edge_index)
    x = x + _L0_ffn_ref(_layernorm(x, axis=-1)[None], L0_ffn_phi, L0_ffn_scale, L0_ffn_w1, L0_ffn_b1, L0_ffn_w2, L0_ffn_b2)[0]
    return x

_drawn_inputs = setup_inputs


def setup_inputs(seed=0):
    import zlib

    import numpy as np

    out = dict(_drawn_inputs(seed))
    spreads = {'L0_gnn_b1': (0.0, 0.1), 'L0_gnn_b2': (0.0, 0.1)}
    factors = {'L0_ffn_phi': 64.0, 'L0_ffn_b1': 48.344, 'L0_ffn_b2': 32.079}
    for name, (base, spread) in spreads.items():
        noise = np.random.default_rng([zlib.crc32(name.encode()), seed]).standard_normal(out[name].shape)
        drawn = base * np.exp(spread * noise) if base else spread * noise
        out[name] = jnp.asarray(drawn.astype(out[name].dtype))
    for name, factor in factors.items():
        out[name] = (out[name] * factor).astype(out[name].dtype)
    return out
```

```python
from contextlib import ExitStack

import concourse.bass as bass
from concourse import mybir

F32 = mybir.dt.float32
F16 = mybir.dt.float16
I32 = mybir.dt.int32
ALU = mybir.AluOpType
ACT = mybir.ActivationFunctionType
AX_X = mybir.AxisListType.X

P = 128
N = 6250
D = 768
E = 100000
DC = D // P
NB = 50
NBR = (N + P - 1) // P
TAIL = N - (NBR - 1) * P
ET = (E + P - 1) // P
EF = E // P
QC = 7
QS = 4
NSTEP = 440
RING = 4
HT = 8
NX = 32
NS = 32
K = NX * NS
H = 384
HC = H // P
KC = K // P
GB = 5
EPS_LN = 1e-5
EPS_L2 = 1e-12
XS = 2.0 ** 10
AS = 2.0 ** -8
US = 2.0 ** 10
PS = 2.0 ** 14
TOP = 2.0 ** 14
assert (ET + 1) // 2 + NBR - 1 <= NSTEP <= QS * P and ET <= QC * P and NSTEP % (2 * RING) == 0


def wait(eng, sem, value):
    if isinstance(value, int) and value <= 0:
        return
    eng.wait_ge(sem, value)


def rounds(eng, n, body, head=1, tail=1):
    for i in range(head):
        body(i)
    with eng.Fori(head, n - tail) as i:
        body(i)
    for i in range(n - tail, n):
        body(i)


def phase_semaphores(nc, ctx):
    sems = []

    def clear():
        nc.clear_and_free_semaphores(sems)
        nc.all_engine_barrier()
    ctx.callback(clear)
    return sems


def exists(b, n):
    return not isinstance(b, int) or 0 <= b < n


class Chain:

    def __init__(self, eng, sem):
        self.eng, self.sem, self.n, self.base = eng, sem, 0, 0

    def at(self, base):
        self.base, self.n = base, 0

    def __call__(self, ins):
        self.n += 1
        ins.then_inc(self.sem, 1)
        self.eng.wait_ge(self.sem, self.base + self.n)


def gnn_ffn(nc, x, src, dst, W1, b1, W2, b2, phi, scale, w1, eb1, w2, eb2, out):
    src_pad = nc.dram_tensor("src_pad", (QC * P, P), I32).ap()
    dst_pad = nc.dram_tensor("dst_pad", (QC * P, P), I32).ap()
    blk_dram = nc.dram_tensor("blk_dram", (QS, P), I32).ap()
    table1 = nc.dram_tensor("table1", (NB * P, 2 * D), F16).ap()
    table2 = nc.dram_tensor("table2", (NB * P, 2 * D), F16).ap()
    x2_dram = nc.dram_tensor("x2_dram", (NB * P, D), F32).ap()
    cw_dram = nc.dram_tensor("cw_dram", (NB * P, 2 * K), F16).ap()

    top = ExitStack()
    with top:
        ident16 = top.enter_context(nc.sbuf_tensor("ident16", [P, P], F16))
        ident32 = top.enter_context(nc.sbuf_tensor("ident32", [P, P], F32))
        ones32 = top.enter_context(nc.sbuf_tensor("ones32", [P, P], F32))
        valid = top.enter_context(nc.sbuf_tensor("valid", [P, NB], F32))
        stats = top.enter_context(nc.sbuf_tensor("stats", [P, NB, 12], F32))
        with ExitStack() as gnn:
            def sb(name, shape, dt):
                return gnn.enter_context(nc.sbuf_tensor(name, shape, dt))

            iota_j = sb("iota_j", [P, P], F16)
            acc = sb("acc", [P, NB, D], F32)
            idx = sb("idx", [P, 2, QS * P], I32)
            dloc = sb("dloc", [P, 2, QS * P], F32)
            blk = sb("blk", [1, QS * P // 4], I32)
            dinv = sb("dinv", [P, NB], F32)
            dinv_as = sb("dinv_as", [P, NB], F32)
            dinv_s2 = sb("dinv_s2", [P, NB], F32)
            lnf = sb("lnf", [P, NB], F32)
            lnb = sb("lnb", [P, NB], F32)
            back = sb("back", [P, 1], F32)
            prepare(nc, x, src, dst, src_pad, dst_pad, blk_dram, acc, idx, dloc, blk, dinv, dinv_as,
                    lnf, lnb, stats, valid, ident16, ident32, ones32, iota_j)
            first_table(nc, acc, lnf, lnb, table1)
            aggregate(nc, "1", table1, acc, idx, dloc, blk, iota_j)
            dense(nc, 1, W1, b1, acc, dinv, dinv_as, dinv_s2, back, stats, ident16, table2, x, x2_dram)
            aggregate(nc, "2", table2, acc, idx, dloc, blk, iota_j)
            dense(nc, 2, W2, b2, acc, dinv, dinv_as, dinv_s2, back, stats, ident16, table2, x, x2_dram)
        with ExitStack() as ffn:
            slots = ffn.enter_context(nc.sbuf_tensor("slots", [P, DC, K], F32))
            dispatch(nc, phi, scale, x2_dram, cw_dram, slots, stats, valid, ident16, ones32)
            with ExitStack() as late:
                eo = late.enter_context(nc.sbuf_tensor("eo", [P, KC, D], F32))
                experts(nc, w1, eb1, w2, eb2, slots, eo, ident32)
                combine(nc, eo, cw_dram, x2_dram, ident16, out)


def prepare(nc, x, src, dst, src_pad, dst_pad, blk_dram, acc, idx, dloc, blk, dinv, dinv_as,
            lnf, lnb, stats, valid, ident16, ident32, ones32, iota_j):
    with ExitStack() as ctx:
        sems = phase_semaphores(nc, ctx)

        def sem(name):
            sems.append(nc.alloc_semaphore(name))
            return sems[-1]

        def sb(name, shape, dt):
            return ctx.enter_context(nc.sbuf_tensor(name, shape, dt))

        def ps(name, shape, dt):
            return ctx.enter_context(nc.psum_tensor(name, shape, dt))

        raw_src = sb("raw_src", [P, 2 * QS, P], I32)
        raw_dst = sb("raw_dst", [P, 2 * QS, P], I32)
        work = sb("work", [P, 2 * QS, P], F32)
        work2 = sb("work2", [P, 2 * QS, P], F32)
        pair_src, pair_dst, fsrc, fdst = (a[:, :, :].rearrange("p (q h) e -> p q (h e)", h=2) for a in (raw_src, raw_dst, work, work2))
        lo16 = sb("lo16", [P, QC * P], F16)
        hi16 = sb("hi16", [P, QC * P], F16)
        iota_b = sb("iota_b", [P, NBR], F16)
        oh_lo = sb("oh_lo", [P, 2, HT, P], F16)
        oh_hi = sb("oh_hi", [P, 2, HT, NBR], F16)
        ones16 = sb("ones16", [P, P], F16)
        zeros16 = sb("zeros16", [P, P], F16)
        diff = sb("diff", [P, P], F32)
        node = sb("node", [P, NB], F32)
        step_k = sb("step_k", [P, QS], F32)
        blk_row = sb("blk_row", [1, QS * P], I32)
        blk_w = sb("blk_w", [1, QS * P // 4], F32)

        b_num = sb("b_num", [P, NBR - 1], F32)
        deg = sb("deg", [P, NB], F32)
        cnt = sb("cnt", [P, NBR], F32)
        ones_b = sb("ones_b", [P, NBR], F32)
        cum = sb("cum", [P, NBR], F32)
        cum_i = sb("cum_i", [P, NBR], I32)
        thr = sb("thr", [P, NBR - 1], F32)
        past = sb("past", [P, QS, NBR - 1], F32)
        bk = sb("bk", [P, QS], F32)
        bk128 = sb("bk128", [P, QS], F32)
        tk = sb("tk", [P, QS], F32)
        tk_i = sb("tk_i", [P, QS], I32)
        bk_i = sb("bk_i", [P, QS], I32)
        mv = sb("mv", [P, NB, 2], F32)
        rstd = sb("rstd", [P, NB], F32)
        psT = ps("psT", [P, 1024], F32)
        psU = ps("psU", [P, 1024], F32)
        psD = ps("psD", [P, 512], F32)
        psC = ps("psC", [P, 512], F32)

        iotas = sem("iotas")
        consts = sem("consts")
        fills = sem("fills")
        edges_in = sem("edges_in")
        edges_out = sem("edges_out")
        x_in = sem("x_in")
        dst_f = sem("dst_f")
        dst_t = sem("dst_t")
        codes = sem("codes")
        lo_ready = sem("lo_ready")
        hi_ready = sem("hi_ready")
        oh_used = sem("oh_used")
        deg_done = sem("deg_done")
        dve = sem("prep_dve")
        deg_read = sem("deg_read")
        rooted = sem("rooted")
        cnt_sum = sem("cnt_sum")
        steps_ready = sem("steps_ready")
        tiles_in = sem("tiles_in")
        tiles_f = sem("tiles_f")
        tiles_t = sem("tiles_t")
        blk_out = sem("blk_out")
        blk_in = sem("blk_in")
        var_ready = sem("var_ready")
        std_ready = sem("std_ready")
        nround = (ET + 2 * HT - 1) // (2 * HT)

        with nc.Block() as block:
            @block.sync
            def _(sp):
                sp.wait_ge(fills, 2)
                full = (QC - 1) * P * P
                for raw, e in ((raw_dst, dst), (raw_src, src)):
                    sp.dma_start(raw[:, 0:QC - 1, :], e[0:full].rearrange("(q p e) -> p q e", p=P, e=P)).then_inc(edges_in, 16)
                    rest = EF - (QC - 1) * P
                    sp.dma_start(raw[0:rest, QC - 1, :], e[full:EF * P].rearrange("(p e) -> p e", e=P)).then_inc(edges_in, 16)
                    sp.dma_start(raw[rest:rest + 1, QC - 1, 0:E - EF * P], e[EF * P:E].rearrange("(p e) -> p e", p=1)).then_inc(edges_in, 16)
                sp.wait_ge(edges_in, 96)
                sp.dma_start(dst_pad.rearrange("(q p) e -> p q e", p=P), raw_dst[:, 0:QC, :]).then_inc(edges_out, 16)
                sp.dma_start(src_pad.rearrange("(q p) e -> p q e", p=P), raw_src[:, 0:QC, :]).then_inc(edges_out, 16)
                sp.wait_ge(fills, 3)
                for c in range(0, NBR - 1, 8):
                    sp.dma_start(acc[:, c:c + 8, :], x[c * P:(c + 8) * P, :].rearrange("(b p) d -> p b d", p=P)).then_inc(x_in, 16)
                sp.dma_start(acc[0:TAIL, NBR - 1, :], x[(NBR - 1) * P:N, :]).then_inc(x_in, 16)
                sp.wait_ge(steps_ready, 1)
                sp.dma_start(blk_dram.rearrange("q p -> p q"), bk_i[:, :], allow_slow_non_contiguous=True).then_inc(blk_out, 16)
                sp.wait_ge(blk_out, 16)
                sp.dma_start(blk_row[:, :], blk_dram.rearrange("(o q) p -> o (q p)", o=1)).then_inc(blk_in, 16)
                sp.wait_ge(blk_in, 16)
                sp.wait_ge(edges_out, 32)

            @block.gpsimd
            def _(pool):
                pool.iota(iota_j[:, :], [[1, P]], base=0, channel_multiplier=0, allow_small_or_imprecise_dtypes=True).then_inc(iotas, 1)
                pool.iota(iota_b[:, :], [[1, NBR]], base=0, channel_multiplier=0, allow_small_or_imprecise_dtypes=True).then_inc(iotas, 1)
                pool.iota(diff[:, :], [[1, P]], base=0, channel_multiplier=-1, allow_small_or_imprecise_dtypes=True).then_inc(iotas, 1)
                pool.iota(node[:, :], [[P, NB]], base=0, channel_multiplier=1, allow_small_or_imprecise_dtypes=True).then_inc(iotas, 1)
                pool.iota(step_k[:, :], [[P, QS]], base=0, channel_multiplier=1, allow_small_or_imprecise_dtypes=True).then_inc(iotas, 1)
                pool.iota(b_num[:, :], [[1, NBR - 1]], base=1, channel_multiplier=0, allow_small_or_imprecise_dtypes=True).then_inc(iotas, 1)
                pool.wait_ge(iotas, 6)
                pool.wait_ge(steps_ready, 2)
                pool.wait_ge(dst_f, 1)
                pool.wait_ge(edges_out, 32)
                for q in range(QS):
                    for pair, pad in ((pair_src, src_pad), (pair_dst, dst_pad)):
                        pool.indirect_dma_start(out=pair[:, q, :], out_offset=None, in_=pad.rearrange("(t h) e -> t (h e)", h=2),
                                                in_offset=bass.IndirectOffsetOnAxis(ap=tk_i[:, q:q + 1], axis=0)).then_inc(tiles_in, 16)

            @block.scalar
            def _(act):
                act.wait_ge(deg_read, 1)
                nc.scalar.activation(dinv[:, 0:NBR], deg[:, 0:NBR], ACT.Sqrt).then_inc(rooted, 1)
                act.wait_ge(var_ready, 1)
                nc.scalar.activation(rstd[:, :], rstd[:, :], ACT.Sqrt).then_inc(std_ready, 1)

            @block.tensor
            def _(pe):
                pe.wait_ge(consts, 5)
                pe.wait_ge(dst_f, 1)
                for q in range(QC):
                    mm = nc.tensor.transpose(psT[:, q * P:(q + 1) * P], work[:, q, :], ident32[:, :])
                mm.then_inc(dst_t, 1)
                nc.tensor.matmul(psD[:, 0:NBR], ident16[:, :], ones16[:, 0:NBR], start=True, stop=False, skip_group_check=True)

                def count(i):
                    for s in range(2):
                        c = 2 * i + s
                        pe.wait_ge(lo_ready, c + 1)
                        pe.wait_ge(hi_ready, c + 1)
                        for t in range(HT):
                            mm = nc.tensor.matmul(psD[:, 0:NBR], oh_lo[:, s, t, :], oh_hi[:, s, t, :], start=False, stop=False, skip_group_check=True)
                        mm.then_inc(oh_used, 1)
                rounds(pe, nround, count)
                nc.tensor.matmul(psD[:, 0:NBR], zeros16[:, :], ones16[:, 0:NBR], start=False, stop=True, skip_group_check=True).then_inc(deg_done, 1)
                pe.wait_ge(deg_read, 2)
                nc.tensor.matmul(psC[:, 0:NBR], ones32[:, :], cnt[:, :], start=True, stop=True).then_inc(cnt_sum, 1)
                pe.wait_ge(tiles_f, 2)
                for h in range(2):
                    for q in range(QS):
                        to = h * QS * P + q * P
                        nc.tensor.transpose(psT[:, to:to + P], fdst[:, q, h * P:(h + 1) * P], ident32[:, :])
                        mm = nc.tensor.transpose(psU[:, to:to + P], fsrc[:, q, h * P:(h + 1) * P], ident32[:, :])
                mm.then_inc(tiles_t, 1)

            @block.vector
            def _(v):
                link = Chain(v, dve)
                v.memset(raw_dst[:, QC - 1, :], -1).then_inc(fills, 1)
                v.memset(raw_src[:, QC - 1, :], 0).then_inc(fills, 1)
                v.memset(acc[:, NBR - 1:NB, :], 0.0).then_inc(fills, 1)
                v.memset(ones16[:, :], 1.0).then_inc(consts, 1)
                v.memset(zeros16[:, :], 0.0).then_inc(consts, 1)
                v.memset(ones32[:, :], 1.0).then_inc(consts, 1)
                v.memset(ones_b[:, :], 1.0)
                v.memset(dinv[:, NBR:NB], 1.0)
                v.wait_ge(iotas, 6)
                v.tensor_scalar(ident16[:, :], diff[:, :], 0.0, None, ALU.is_equal).then_inc(consts, 1)
                v.tensor_scalar(ident32[:, :], diff[:, :], 0.0, None, ALU.is_equal).then_inc(consts, 1)
                v.tensor_scalar(valid[:, :], node[:, :], float(N), None, ALU.is_lt)
                v.wait_ge(edges_in, 96)
                v.tensor_copy(work[:, 0:QC, :], raw_dst[:, 0:QC, :]).then_inc(dst_f, 1)
                v.wait_ge(dst_t, 1)
                link(v.tensor_copy(as_int(work), psT[:, 0:QC * P]))
                wi = as_int(work)
                w2i = as_int(work2)
                link(v.tensor_scalar(w2i, wi, 127, None, ALU.bitwise_and))
                v.tensor_copy(lo16[:, :], w2i).then_inc(codes, 1)
                v.wait_ge(codes, 1)
                link(v.tensor_scalar(w2i, wi, 7, None, ALU.arith_shift_right))
                v.tensor_copy(hi16[:, :], w2i).then_inc(codes, 1)
                v.wait_ge(codes, 2)

                def hot_nodes(i):
                    for s in range(2):
                        c = 2 * i + s
                        wait(v, oh_used, c - 1)
                        v.tensor_tensor(
                            oh_lo[:, s], iota_j[:, :].unsqueeze(1).to_broadcast([P, HT, P]),
                            lo16[:, bass.ds(c * HT, HT)].unsqueeze(2).to_broadcast([P, HT, P]), ALU.is_equal).then_inc(lo_ready, 1)
                        v.tensor_tensor(
                            oh_hi[:, s], iota_b[:, :].unsqueeze(1).to_broadcast([P, HT, NBR]),
                            hi16[:, bass.ds(c * HT, HT)].unsqueeze(2).to_broadcast([P, HT, NBR]), ALU.is_equal).then_inc(hi_ready, 1)
                rounds(v, nround, hot_nodes)
                v.wait_ge(x_in, 16 * 7)
                with v.Fori(0, NB) as b:
                    for h in range(2):
                        v.bn_stats(stats[:, bass.ds(b, 1), 6 * h:6 * h + 6], acc[:, bass.ds(b, 1), h * 384:(h + 1) * 384]).then_inc(dve, 1)
                v.wait_ge(dve, 3 + 2 * NB)
                link.n = 3 + 2 * NB
                for b in range(NB):
                    v.bn_aggr(mv[:, b, :], stats[:, b, :]).then_inc(dve, 1)
                link.n += NB
                v.wait_ge(dve, link.n)
                v.tensor_scalar(rstd[:, :], mv[:, :, 1], EPS_LN, None, ALU.add).then_inc(var_ready, 1)
                v.wait_ge(deg_done, 1)
                v.tensor_copy(deg[:, 0:NBR], psD[:, 0:NBR]).then_inc(deg_read, 1)
                v.wait_ge(deg_read, 1)
                v.tensor_scalar(cnt[:, :], deg[:, 0:NBR], -1.0, None, ALU.add).then_inc(deg_read, 1)
                v.wait_ge(rooted, 1)
                link(v.reciprocal(dinv[:, 0:NBR], dinv[:, 0:NBR]))
                v.tensor_scalar(dinv_as[:, :], dinv[:, :], AS, None, ALU.mult)
                v.wait_ge(std_ready, 1)
                link(v.reciprocal(rstd[:, :], rstd[:, :]))
                link(v.scalar_tensor_tensor(lnf[:, :], rstd[:, :], XS, dinv[:, :], ALU.mult, ALU.mult))
                v.scalar_tensor_tensor(lnb[:, :], mv[:, :, 0], -1.0, lnf[:, :], ALU.mult, ALU.mult)
                v.wait_ge(cnt_sum, 1)
                link(v.tensor_tensor_scan(cum[:, :], ones_b[:, :], psC[:, 0:NBR], 0.0, ALU.mult, ALU.add))
                link(v.tensor_copy(cum_i[:, :], cum[:, :]))
                link(v.tensor_scalar(cum_i[:, :], cum_i[:, :], 8, None, ALU.arith_shift_right))
                link(v.tensor_copy(cum[:, :], cum_i[:, :]))
                link(v.tensor_tensor(thr[:, :], cum[:, 0:NBR - 1], b_num[:, :], ALU.add))
                link(v.tensor_tensor(past[:, :, :], step_k[:, :].unsqueeze(2).to_broadcast([P, QS, NBR - 1]),
                                     thr[:, :].unsqueeze(1).to_broadcast([P, QS, NBR - 1]), ALU.is_ge))
                link(v.tensor_reduce(bk[:, :], past[:, :, :], AX_X, ALU.add))
                v.tensor_copy(bk_i[:, :], bk[:, :]).then_inc(steps_ready, 1)
                link(v.tensor_scalar(bk128[:, :], bk[:, :], float(P), None, ALU.mult))
                link(v.tensor_tensor(tk[:, :], step_k[:, :], bk[:, :], ALU.subtract))
                link(v.tensor_scalar(tk[:, :], tk[:, :], float(QC * P // 2 - 1), None, ALU.min))
                v.wait_ge(steps_ready, 1)
                v.tensor_copy(tk_i[:, :], tk[:, :]).then_inc(steps_ready, 1)
                v.wait_ge(tiles_in, 16 * 2 * QS)
                for q in range(QS):
                    last = v.tensor_scalar(fdst[:, q, :], pair_dst[:, q, :], bk128[:, q:q + 1], None, ALU.subtract)
                last.then_inc(tiles_f, 1)
                v.tensor_copy(fsrc[:, :, :], pair_src[:, :, :]).then_inc(tiles_f, 1)
                v.wait_ge(blk_in, 16)
                four = blk_row[:, :].rearrange("o (m r) -> o m r", r=4)
                link(v.tensor_copy(blk_w[:, :], four[:, :, 0]))
                for r in range(1, 4):
                    link(v.scalar_tensor_tensor(blk_w[:, :], four[:, :, r], float(64 ** r), blk_w[:, :], ALU.mult, ALU.add))
                v.tensor_copy(blk[:, :], blk_w[:, :])
                v.wait_ge(tiles_t, 1)
                v.tensor_copy(dloc[:, :, :].rearrange("p h k -> p (h k)"), psT[:, 0:2 * QS * P])
                v.tensor_copy(idx[:, :, :].rearrange("p h k -> p (h k)"), psU[:, 0:2 * QS * P])


def as_int(work):
    return work[:, 0:QC, :].rearrange("p q e -> p (q e)").bitcast(I32)


def first_table(nc, acc, lnf, lnb, table):
    with ExitStack() as ctx:
        sems = phase_semaphores(nc, ctx)

        def sem(name):
            sems.append(nc.alloc_semaphore(name))
            return sems[-1]

        TR = 5
        stage = ctx.enter_context(nc.sbuf_tensor("stage", [P, TR, 2 * D], F16))
        hi_ready = sem("t1_hi")
        acc_ready = sem("t1_acc")
        lo_ready = sem("t1_lo")
        stored = [sem(f"t1_st{s}") for s in range(TR)]
        tick = sem("t1_tick")
        n = NB // TR
        with nc.Block() as block:
            @block.scalar
            def _(act):
                def body(i):
                    for s in range(TR):
                        b = TR * i + s
                        wait(act, stored[s], 16 * i)
                        act.sem_inc(tick, 1)
                        f, c = lnf[:, bass.ds(b, 1)], lnb[:, bass.ds(b, 1)]
                        rows = acc[:, bass.ds(b, 1), :].rearrange("p o d -> p (o d)")
                        nc.scalar.activation(stage[:, s, 0:D], rows, ACT.Identity, bias=c, scale=f).then_inc(hi_ready, 1)
                rounds(act, n, body)

            @block.vector
            def _(v):
                def body(i):
                    for s in range(TR):
                        b = TR * i + s
                        v.wait_ge(hi_ready, b + 1)
                        wait(v, stored[s], 16 * i)
                        rows = acc[:, bass.ds(b, 1), :].rearrange("p o d -> p (o d)")
                        v.tensor_scalar(rows, rows, lnf[:, bass.ds(b, 1)], lnb[:, bass.ds(b, 1)], ALU.mult, ALU.add).then_inc(acc_ready, 1)
                        v.wait_ge(acc_ready, b + 1)
                        v.tensor_tensor(stage[:, s, D:2 * D], rows, stage[:, s, 0:D], ALU.subtract).then_inc(lo_ready, 1)
                rounds(v, n, body)

            @block.sync
            def _(sp):
                def body(i):
                    for s in range(TR):
                        b = TR * i + s
                        sp.wait_ge(hi_ready, b + 1)
                        sp.wait_ge(lo_ready, b + 1)
                        sp.dma_start(table[bass.ds(b * P, P), :], stage[:, s, :]).then_inc(stored[s], 16)
                rounds(sp, n, body)
                for s in range(TR):
                    sp.wait_ge(stored[s], 16 * n)


def aggregate(nc, tag, table, acc, idx, dloc, blk, iota_j):
    with ExitStack() as ctx:
        sems = phase_semaphores(nc, ctx)

        def sem(name):
            sems.append(nc.alloc_semaphore(name))
            return sems[-1]

        ring = ctx.enter_context(nc.sbuf_tensor("ring" + tag, [P, RING, 2, 2 * D], F16))
        pick = ctx.enter_context(nc.sbuf_tensor("pick" + tag, [P, RING, 2, P], F16))
        rows_i = ctx.enter_context(nc.sbuf_tensor("rows_i" + tag, [P, 2, 2, RING], I32))
        part = ctx.enter_context(nc.psum_tensor("part" + tag, [P, 4, 1024], F32))
        gathered = [sem(f"gathered{tag}_{r}") for r in range(2 * RING)]
        rows_r = sem("rows_r" + tag)
        picked = sem("picked" + tag)
        summed = sem("summed" + tag)
        added = sem("added" + tag)
        tick = sem("ag_tick" + tag)
        R2 = 2 * RING
        n = NSTEP // R2
        with nc.Block() as block:
            @block.scalar
            def _(act):
                def body(i):
                    for u in range(2):
                        wait(act, summed, R2 * i + RING * (u - 1))
                        act.sem_inc(tick, 1)
                        nc.scalar.copy(rows_i[:, u], idx[:, :, bass.ds(R2 * i + RING * u, RING)]).then_inc(rows_r, 1)
                rounds(act, n, body)

            @block.gpsimd
            def _(pool):
                def body(i):
                    for r in range(R2):
                        k = R2 * i + r
                        u, q = r // RING, r % RING
                        if q == 0:
                            pool.wait_ge(rows_r, 2 * i + u + 1)
                            pool.sem_inc(tick, 1)
                        if exists(k - RING, NSTEP):
                            pool.wait_ge(summed, k - RING + 1)
                            pool.sem_inc(tick, 1)
                        for h in range(2):
                            pool.indirect_dma_start(out=ring[:, q, h, :], out_offset=None, in_=table,
                                                    in_offset=bass.IndirectOffsetOnAxis(ap=rows_i[:, u, h, q:q + 1], axis=0)).then_inc(gathered[2 * q + h], 16)
                rounds(pool, n, body)

            @block.tensor
            def _(pe):
                def body(i):
                    for r in range(R2):
                        k = R2 * i + r
                        q = r % RING
                        pe.wait_ge(picked, k + 1)
                        wait(pe, added, k - 3)
                        for h in range(2):
                            pe.wait_ge(gathered[2 * q + h], 16 * (2 * i + r // RING + 1))
                            for half in range(2):
                                for a, z in ((0, 512), (512, D)):
                                    mm = nc.tensor.matmul(part[:, r % 4, a:z], pick[:, q, h, :], ring[:, q, h, half * D + a:half * D + z],
                                                          start=(h == 0 and half == 0), stop=(h == 1 and half == 1))
                        mm.then_inc(summed, 1)
                rounds(pe, n, body)

            @block.vector
            def _(v):
                def add(k, b, s):
                    wait(v, added, k)
                    v.wait_ge(summed, k + 1)
                    rows = acc[:, bass.ds(b, 1), :].rearrange("p o d -> p (o d)")
                    v.tensor_tensor(rows, rows, part[:, s, 0:D], ALU.add).then_inc(added, 1)

                def blocks(word):
                    w = v.value_load(blk[0:1, bass.ds(word, 1)])
                    return [((w >> (6 * r)) & 63).with_bounds(min_val=0, max_val=NBR - 1) for r in range(4)]

                def body(i):
                    for u in range(2):
                        if u or exists(i - 1, n):
                            old = blocks(2 * i + u - 1)
                        new = blocks(2 * i + u)
                        for q in range(RING):
                            k = R2 * i + RING * u + q
                            wait(v, summed, k - RING + 1)
                            v.tensor_tensor(pick[:, q], iota_j[:, :].unsqueeze(1).to_broadcast([P, 2, P]),
                                            dloc[:, :, bass.ds(k, 1)].to_broadcast([P, 2, P]), ALU.is_equal).then_inc(picked, 1)
                            if exists(k - 2, NSTEP):
                                add(k - 2, new[q - 2] if q >= 2 else old[q + 2], (q - 2) % 4)
                rounds(v, n, body)
                last = blocks(NSTEP // 4 - 1)
                for k in range(NSTEP - 2, NSTEP):
                    add(k, last[k % 4], k % 4)


def power_scale(nc, v, link, val, pw, sc, inv, top):
    link(v.tensor_scalar(val, val, 1e-20, None, ALU.max))
    link(v.tensor_scalar(pw.bitcast(I32), val.bitcast(I32), 0x7F800000, None, ALU.bitwise_and))
    link(v.reciprocal(sc, pw))
    link(v.tensor_scalar(sc, sc, top, None, ALU.mult))
    link(v.tensor_scalar(inv, pw, 1.0 / top, None, ALU.mult))


def dense(nc, layer, W, bias, acc, dinv, dinv_as, dinv_s2, back, stats, ident16, table2, x, x2_dram):
    g = f"d{layer}_"
    with ExitStack() as ctx:
        sems = phase_semaphores(nc, ctx)

        def sem(name):
            sems.append(nc.alloc_semaphore(name))
            return sems[-1]

        def sb(name, shape, dt):
            return ctx.enter_context(nc.sbuf_tensor(g + name, shape, dt))

        Wh = sb("Wh", [P, DC, D], F16)
        Wl = sb("Wl", [P, DC, D], F16)
        brow = sb("brow", [P, D], F32)
        inv = sb("inv", [P, 1], F32)
        with ExitStack() as pre:
            def sbp(name, shape, dt):
                return pre.enter_context(nc.sbuf_tensor(g + name, shape, dt))
            Wf = sbp("Wf", [P, DC, D], F32)
            mx = sbp("mx", [P, 1], F32)
            bm = sbp("bm", [P, 1], F32)
            wm = sbp("wm", [P, 1], F32)
            pw = sbp("pw", [P, 1], F32)
            sc = sbp("sc", [P, 1], F32)
            s2 = sbp("s2", [P, 1], F32)
            w_in, maxed, allmax, scaled, dve, hi = (sem(g + n) for n in ("w_in", "maxed", "allmax", "scaled", "dve", "hi"))
            with nc.Block() as block:
                @block.sync
                def _(sp):
                    sp.dma_start(Wf[:, :, :], W.rearrange("(c p) n -> p c n", p=P)).then_inc(w_in, 16)
                    sp.dma_start(brow[:, :], bias.rearrange("(o d) -> o d", o=1).to_broadcast([P, D])).then_inc(w_in, 16)

                @block.gpsimd
                def _(pool):
                    pool.wait_ge(maxed, 1)
                    pool.partition_all_reduce(wm[:, :], mx[:, :], P, bass.bass_isa.ReduceOp.max).then_inc(allmax, 1)

                @block.vector
                def _(v):
                    link = Chain(v, dve)
                    v.wait_ge(w_in, 32)
                    v.tensor_reduce(mx[:, :], Wf[:, :, :].rearrange("p c n -> p (c n)"), AX_X, ALU.max, apply_absolute_value=True).then_inc(maxed, 1)
                    link(v.tensor_reduce(bm[:, :], brow[:, :], AX_X, ALU.max, apply_absolute_value=True))
                    v.wait_ge(allmax, 1)
                    link(v.scalar_tensor_tensor(bm[:, :], wm[:, :], float(D), bm[:, :], ALU.mult, ALU.add))
                    power_scale(nc, v, link, wm[:, :], pw[:, :], sc[:, :], inv[:, :], TOP)
                    v.nop().then_inc(scaled, 1)
                    if layer == 1:
                        link(v.tensor_scalar(inv[:, :], inv[:, :], 1.0 / (XS * AS), None, ALU.mult))
                        power_scale(nc, v, link, bm[:, :], pw[:, :], s2[:, :], back[:, :], TOP)
                        link(v.tensor_scalar(dinv_s2[:, :], dinv[:, :], s2[:, 0:1], None, ALU.mult))
                    else:
                        link(v.tensor_scalar(inv[:, :], inv[:, :], 1.0 / AS, None, ALU.mult))
                        link(v.tensor_tensor(inv[:, :], inv[:, :], back[:, :], ALU.mult))
                    v.wait_ge(hi, 1)
                    v.scalar_tensor_tensor(Wl[:, :, :].rearrange("p c n -> p (c n)"), Wf[:, :, :].rearrange("p c n -> p (c n)"), sc[:, 0:1],
                                           Wh[:, :, :].rearrange("p c n -> p (c n)"), ALU.mult, ALU.subtract)

                @block.scalar
                def _(act):
                    act.wait_ge(scaled, 1)
                    nc.scalar.activation(Wh[:, :, :], Wf[:, :, :], ACT.Copy, scale=sc[:, 0:1]).then_inc(hi, 1)

        v2 = sb("v2", [P, 2, 2, D], F16)
        vT = sb("vT", [P, 2, 2, D], F16)
        h = sb("h", [P, D], F32)
        ps_t = [ctx.enter_context(nc.psum_tensor(f"{g}pt{i}", [P, 2, 1024], F16)) for i in range(2)]
        ps_o = ctx.enter_context(nc.psum_tensor(g + "po", [P, 2, 1024], F32))
        hi_ready, lo_ready, turned, hi_back, lo_back, prod, biased, tick = (
            sem(g + n) for n in ("hi_ready", "lo_ready", "turned", "hi_back", "lo_back", "prod", "biased", "tick"))
        hi_out, acc_out, lo_out, stats_r = (sem(g + n) for n in ("hi_out", "acc_out", "lo_out", "stats_r"))
        stored = [sem(g + "st0"), sem(g + "st1")]
        x_in = [sem(g + "x0"), sem(g + "x1")]
        if layer == 1:
            stage = sb("stage", [P, 2, 2 * D], F16)
        else:
            xb = sb("xb", [P, 2, D], F32)
        n = NB // 2 + 1

        def rows_of(b):
            return acc[:, bass.ds(b, 1), :].rearrange("p o d -> p (o d)")

        with nc.Block() as block:
            @block.scalar
            def _(act):
                def body(j):
                    for s in range(2):
                        i = 2 * j + s
                        if exists(i, NB):
                            wait(act, turned, i - 1)
                            act.sem_inc(tick, 1)
                            nc.scalar.activation(v2[:, s, 0, :], rows_of(i), ACT.Copy, scale=dinv_as[:, bass.ds(i, 1)]).then_inc(hi_ready, 1)
                        if exists(i - 1, NB):
                            act.wait_ge(turned, i)
                            wait(act, prod, i - 2)
                            nc.scalar.activation(vT[:, 1 - s, 0, :], ps_t[1 - s][:, 0, 0:D], ACT.Copy).then_inc(hi_back, 1)
                        if exists(i - 2, NB) and layer == 1:
                            b = i - 2
                            act.wait_ge(biased, b + 1)
                            wait(act, stored[s], 16 * (j - 1))
                            act.sem_inc(tick, 1)
                            f = dinv_s2[:, bass.ds(b, 1)]
                            nc.scalar.activation(stage[:, s, 0:D], h[:, :], ACT.Relu, scale=f).then_inc(hi_out, 1)
                            nc.scalar.activation(rows_of(b), h[:, :], ACT.Relu, scale=f).then_inc(acc_out, 1)
                rounds(act, n, body, head=2)

            @block.vector
            def _(v):
                def body(j):
                    for s in range(2):
                        i = 2 * j + s
                        if exists(i, NB):
                            v.wait_ge(hi_ready, i + 1)
                            wait(v, turned, i - 1)
                            v.scalar_tensor_tensor(v2[:, s, 1, :], rows_of(i), dinv_as[:, bass.ds(i, 1)], v2[:, s, 0, :],
                                                   ALU.mult, ALU.subtract).then_inc(lo_ready, 1)
                        if exists(i - 1, NB):
                            v.wait_ge(turned, i)
                            wait(v, prod, i - 2)
                            v.tensor_copy(vT[:, 1 - s, 1, :], ps_t[1 - s][:, 1, 0:D]).then_inc(lo_back, 1)
                        if exists(i - 2, NB):
                            b = i - 2
                            v.wait_ge(prod, b + 1)
                            if layer == 1:
                                wait(v, acc_out, b)
                            v.scalar_tensor_tensor(h[:, :], ps_o[:, s, 0:D], inv[:, 0:1], brow[:, :], ALU.mult, ALU.add).then_inc(biased, 1)
                            if layer == 1:
                                v.wait_ge(hi_out, b + 1)
                                v.wait_ge(acc_out, b + 1)
                                wait(v, stored[s], 16 * (j - 1))
                                v.tensor_tensor(stage[:, s, D:2 * D], rows_of(b), stage[:, s, 0:D], ALU.subtract).then_inc(lo_out, 1)
                            else:
                                v.wait_ge(biased, b + 1)
                                v.wait_ge(x_in[s], 16 * j)
                                v.tensor_tensor(xb[:, s, :], h[:, :], xb[:, s, :], ALU.add).then_inc(lo_out, 1)
                                v.wait_ge(lo_out, b + 1)
                                v.sem_inc(tick, 1)
                                for q in range(2):
                                    st = v.bn_stats(stats[:, bass.ds(b, 1), 6 * q:6 * q + 6], xb[:, s, q * (D // 2):(q + 1) * (D // 2)])
                                st.then_inc(stats_r, 1)
                rounds(v, n, body, head=2)

            @block.tensor
            def _(pe):
                def body(j):
                    for s in range(2):
                        i = 2 * j + s
                        if exists(i - 1, NB):
                            t = 1 - s
                            pe.wait_ge(hi_ready, i)
                            pe.wait_ge(lo_ready, i)
                            wait(pe, hi_back, i - 2)
                            wait(pe, lo_back, i - 2)
                            for half in range(2):
                                for c in range(DC):
                                    mm = nc.tensor.transpose(ps_t[t][:, half, c * P:(c + 1) * P], v2[:, t, half, c * P:(c + 1) * P], ident16[:, :])
                            mm.then_inc(turned, 1)
                        if exists(i - 2, NB):
                            b = i - 2
                            pe.wait_ge(hi_back, b + 1)
                            pe.wait_ge(lo_back, b + 1)
                            wait(pe, biased, b - 1)
                            for c in range(DC):
                                for half, Ws in ((0, (Wh, Wl)), (1, (Wh,))):
                                    for Wp in Ws:
                                        for a, z in ((0, 512), (512, D)):
                                            mm = nc.tensor.matmul(ps_o[:, s, a:z], vT[:, s, half, c * P:(c + 1) * P], Wp[:, c, a:z],
                                                                  start=(c == 0 and half == 0 and Wp is Wh), stop=(c == DC - 1 and half == 1))
                            mm.then_inc(prod, 1)
                rounds(pe, n, body, head=2)

            @block.sync
            def _(sp):
                def body(j):
                    for s in range(2):
                        b = 2 * j + s - 2
                        if exists(b, NB):
                            sp.wait_ge(lo_out, b + 1)
                            if layer == 1:
                                sp.wait_ge(hi_out, b + 1)
                                sp.dma_start(table2[bass.ds(b * P, P), :], stage[:, s, :]).then_inc(stored[s], 16)
                            else:
                                sp.dma_start(x2_dram[bass.ds(b * P, P), :], xb[:, s, :]).then_inc(stored[s], 16)
                        if layer == 2 and exists(b + 2, NB):
                            rows, r0 = P, (b + 2) * P
                            if isinstance(b, int) and b + 2 == NBR - 1:
                                rows = TAIL
                            elif isinstance(b, int) and b + 2 >= NBR:
                                r0 = 0
                            wait(sp, stored[s], 16 * j)
                            if not isinstance(b, int) or b >= 0:
                                wait(sp, stats_r, b + 1)
                            sp.dma_start(xb[0:rows, s, :], x[bass.ds(r0, rows), :]).then_inc(x_in[s], 16)
                rounds(sp, n, body, head=2, tail=2)
                for s in range(2):
                    sp.wait_ge(stored[s], 16 * (n - 1))



def dispatch(nc, phi, scale, x2_dram, cw_dram, slots, stats, valid, ident16, ones32):
    with ExitStack() as ctx:
        sems = phase_semaphores(nc, ctx)

        def sem(name):
            sems.append(nc.alloc_semaphore(name))
            return sems[-1]

        def sb(name, shape, dt):
            return ctx.enter_context(nc.sbuf_tensor("s_" + name, shape, dt))

        phi_h = sb("phi_h", [P, DC, K], F16)
        phi_l = sb("phi_l", [P, DC, K], F16)
        scl = sb("scl", [P, 1], F32)
        xf = sb("xf", [P, NB], F32)
        xc = sb("xc", [P, NB], F32)
        with ExitStack() as pre:
            def sbp(name, shape, dt):
                return pre.enter_context(nc.sbuf_tensor("s_" + name, shape, dt))
            phi_f = sbp("phi_f", [P, DC, K], F32)
            sq = sbp("sq", [P, DC, K], F32)
            norm = sbp("norm", [P, K], F32)
            mv = sbp("mv", [P, NB, 2], F32)
            var = sbp("var", [P, 2, NB], F32)
            ps_n = pre.enter_context(nc.psum_tensor("s_ps_n", [P, 1024], F32))
            p_in, squared, normed, rooted, unit, hi, agg, var_r, std_r, dve = (
                sem("p_" + n) for n in ("p_in", "squared", "normed", "rooted", "unit", "hi", "agg", "var_r", "std_r", "dve"))
            with nc.Block() as block:
                @block.sync
                def _(sp):
                    sp.dma_start(phi_f[:, :, :], phi.rearrange("(c p) e s -> p c (e s)", p=P)).then_inc(p_in, 16)
                    sp.dma_start(scl[:, :], scale.rearrange("(o d) -> o d", o=1).to_broadcast([P, 1])).then_inc(p_in, 16)

                @block.tensor
                def _(pe):
                    pe.wait_ge(squared, 1)
                    for a in (0, 512):
                        for c in range(DC):
                            mm = nc.tensor.matmul(ps_n[:, a:a + 512], ones32[:, :], sq[:, c, a:a + 512], start=(c == 0), stop=(c == DC - 1))
                    mm.then_inc(normed, 1)

                @block.scalar
                def _(act):
                    act.wait_ge(var_r, 2)
                    nc.scalar.activation(var[:, :, :], var[:, :, :], ACT.Sqrt).then_inc(std_r, 1)
                    act.wait_ge(normed, 1)
                    nc.scalar.activation(norm[:, :], ps_n[:, :], ACT.Sqrt).then_inc(rooted, 1)
                    act.wait_ge(unit, 1)
                    nc.scalar.activation(phi_h[:, :, :], phi_f[:, :, :], ACT.Copy, scale=US).then_inc(hi, 1)

                @block.vector
                def _(v):
                    link = Chain(v, dve)
                    for b in range(NB):
                        last = v.bn_aggr(mv[:, b, :], stats[:, b, :])
                        last.then_inc(agg, 1)
                    v.wait_ge(agg, NB)
                    v.tensor_scalar(var[:, 0, :], mv[:, :, 1], EPS_LN, None, ALU.add).then_inc(var_r, 1)
                    v.tensor_scalar(var[:, 1, :], mv[:, :, 1], float(D), None, ALU.mult).then_inc(var_r, 1)
                    v.wait_ge(p_in, 32)
                    v.tensor_tensor(sq[:, :, :], phi_f[:, :, :], phi_f[:, :, :], ALU.mult).then_inc(squared, 1)
                    link(v.tensor_scalar(scl[:, :], scl[:, :], 1.0 / (US * US), None, ALU.mult))
                    v.wait_ge(std_r, 1)
                    link(v.reciprocal(var[:, 0, :], var[:, 0, :]))
                    link(v.tensor_tensor(var[:, 1, :], var[:, 1, :], var[:, 0, :], ALU.mult))
                    link(v.tensor_scalar(var[:, 1, :], var[:, 1, :], EPS_L2, None, ALU.max))
                    link(v.reciprocal(var[:, 1, :], var[:, 1, :]))
                    link(v.scalar_tensor_tensor(xf[:, :], var[:, 0, :], US, var[:, 1, :], ALU.mult, ALU.mult))
                    link(v.tensor_tensor(xf[:, :], xf[:, :], valid[:, :], ALU.mult))
                    link(v.scalar_tensor_tensor(xc[:, :], mv[:, :, 0], -1.0, xf[:, :], ALU.mult, ALU.mult))
                    v.wait_ge(rooted, 1)
                    link(v.tensor_scalar(norm[:, :], norm[:, :], EPS_L2, None, ALU.max))
                    link(v.reciprocal(norm[:, :], norm[:, :]))
                    v.tensor_tensor(phi_f[:, :, :], phi_f[:, :, :], norm[:, :].unsqueeze(1).to_broadcast([P, DC, K]), ALU.mult).then_inc(unit, 1)
                    v.wait_ge(unit, 1)
                    v.wait_ge(hi, 1)
                    v.scalar_tensor_tensor(phi_l[:, :, :].rearrange("p c n -> p (c n)"), phi_f[:, :, :].rearrange("p c n -> p (c n)"), US,
                                           phi_h[:, :, :].rearrange("p c n -> p (c n)"), ALU.mult, ALU.subtract)

        RB = 2 * GB
        xin = sb("xin", [P, 2, D], F32)
        xn = sb("xn", [P, RB, 2, D], F16)
        xT = sb("xT", [P, 2, 2, D], F16)
        lg = sb("lg", [P, 2, K], F32)
        dwf = sb("dwf", [P, 2, K], F32)
        cwf = sb("cwf", [P, 2, K], F32)
        dw = sb("dw", [P, RB, 2, K], F16)
        cst = sb("cst", [P, 2, 2 * K], F16)
        m = sb("m", [P, 2, NX], F32)
        nM = sb("nM", [P, 2], F32)
        em = sb("em", [P, 2, NX], F32)
        z = sb("z", [P, 2, NX], F32)
        rz = sb("rz", [P, 2, NX], F32)
        wz = sb("wz", [P, 2, NX], F32)
        Z = sb("Z", [P, 2], F32)
        g = sb("g", [P, 2, NX], F32)
        ps_t = ctx.enter_context(nc.psum_tensor("s_pt", [P, 2, 1024], F16))
        ps_l = ctx.enter_context(nc.psum_tensor("s_pl", [P, 2, 1024], F32))
        ps_s = ctx.enter_context(nc.psum_tensor("s_ps", [P, 2, 512], F32))
        (xn_hi, xn_f, xn_lo, turned, hi_back, lo_back, logits, scaled, maxed, shifted, em_r, expd, dwf_r, g_r, dw_hi,
         dw_lo, cwf_r, cw_hi, cw_lo, tiles, added, dve, tick) = (sem("m_" + n) for n in (
             "xn_hi", "xn_f", "xn_lo", "turned", "hi_back", "lo_back", "logits", "scaled", "maxed", "shifted", "em_r", "expd",
             "dwf_r", "g_r", "dw_hi", "dw_lo", "cwf_r", "cw_hi", "cw_lo", "tiles", "added", "dve", "tick"))
        x_in = [sem("m_x0"), sem("m_x1")]
        stored = [sem("m_st0"), sem("m_st1")]
        NT = 2 * DC
        LINKS = 7
        n = (NB + GB) // RB + 1

        def by_expert(ap):
            return ap.rearrange("p (e s) -> p e s", s=NS)

        def group_of(j, s):
            gr, u = (2 * j, s - GB - 2) if s >= GB else (2 * j - 1, s - 2)
            return (gr, 4 * u) if 0 <= u < 3 and exists(gr, NB // GB) else (None, 0)

        with nc.Block() as block:
            @block.sync
            def _(sp):
                def body(j):
                    for s in range(RB):
                        i = RB * j + s
                        if exists(i, NB):
                            wait(sp, xn_lo, i - 1)
                            sp.dma_start(xin[:, s % 2, :], x2_dram[bass.ds(i * P, P), :]).then_inc(x_in[s % 2], 16)
                        b = i - 3
                        if exists(b, NB):
                            sp.wait_ge(cw_hi, b + 1)
                            sp.wait_ge(cw_lo, b + 1)
                            sp.dma_start(cw_dram[bass.ds(b * P, P), :], cst[:, (s - 3) % 2, :]).then_inc(stored[(s - 3) % 2], 16)
                rounds(sp, n, body)
                for s in range(2):
                    sp.wait_ge(stored[s], 16 * (NB // 2))

            @block.scalar
            def _(act):
                def body(j):
                    for s in range(RB):
                        i = RB * j + s
                        t = s % 2
                        if exists(i, NB):
                            act.wait_ge(x_in[t], 16 * (GB * j + s // 2 + 1))
                            wait(act, tiles, NT * (2 * j + s // GB - 1))
                            act.sem_inc(tick, 1)
                            f, c = xf[:, bass.ds(i, 1)], xc[:, bass.ds(i, 1)]
                            nc.scalar.activation(xn[:, s, 0, :], xin[:, t, :], ACT.Identity, bias=c, scale=f).then_inc(xn_hi, 1)
                            nc.scalar.activation(xin[:, t, :], xin[:, t, :], ACT.Identity, bias=c, scale=f).then_inc(xn_f, 1)
                        if exists(i - 1, NB):
                            act.wait_ge(turned, i)
                            wait(act, logits, i - 2)
                            nc.scalar.activation(xT[:, 1 - t, 0, :], ps_t[:, 0, 0:D], ACT.Copy).then_inc(hi_back, 1)
                        b = i - 2
                        if exists(b, NB):
                            act.wait_ge(logits, b + 1)
                            wait(act, dwf_r, b - 1)
                            nc.scalar.activation(lg[:, t, :], ps_l[:, t, :], ACT.Copy, scale=scl[:, 0:1]).then_inc(scaled, 1)
                            act.wait_ge(maxed, b + 1)
                            wait(act, g_r, b - 1)
                            nc.scalar.activation(em[:, t, :], m[:, t, :], ACT.Exp, bias=nM[:, t:t + 1]).then_inc(em_r, 1)
                            act.wait_ge(shifted, b + 1)
                            nc.scalar.activation(lg[:, t, :], lg[:, t, :], ACT.Exp).then_inc(expd, 1)
                            act.wait_ge(dwf_r, b + 1)
                            nc.scalar.activation(dw[:, (s - 2) % RB, 0, :], dwf[:, t, :], ACT.Copy).then_inc(dw_hi, 1)
                            act.wait_ge(cwf_r, b + 1)
                            wait(act, stored[t], 16 * (GB * j + s // 2 - 1))
                            nc.scalar.activation(cst[:, t, 0:K], cwf[:, t, :], ACT.Copy).then_inc(cw_hi, 1)
                rounds(act, n, body)

            @block.vector
            def _(v):
                link = Chain(v, dve)

                def add(gr, u):
                    tile = NT * gr + u
                    v.wait_ge(tiles, tile + 1)
                    c, a = u // 2, 512 * (u % 2)
                    dst_s = slots[:, c, a:a + 512]
                    if isinstance(gr, int) and gr == 0:
                        v.tensor_copy(dst_s, ps_s[:, u % 2, :]).then_inc(added, 1)
                    else:
                        wait(v, added, tile - NT + 1)
                        v.tensor_tensor(dst_s, dst_s, ps_s[:, u % 2, :], ALU.add).then_inc(added, 1)

                def body(j):
                    for s in range(RB):
                        i = RB * j + s
                        t = s % 2
                        gr, u0 = group_of(j, s)
                        if exists(i, NB):
                            v.wait_ge(xn_hi, i + 1)
                            v.wait_ge(xn_f, i + 1)
                            v.tensor_tensor(xn[:, s, 1, :], xin[:, t, :], xn[:, s, 0, :], ALU.subtract).then_inc(xn_lo, 1)
                        if exists(i - 1, NB):
                            v.wait_ge(turned, i)
                            wait(v, logits, i - 2)
                            v.tensor_copy(xT[:, 1 - t, 1, :], ps_t[:, 1, 0:D]).then_inc(lo_back, 1)
                        b = i - 2
                        if exists(b, NB):
                            link.at(LINKS * b)
                            v.wait_ge(scaled, b + 1)
                            wait(v, em_r, b - 1)
                            link(v.tensor_reduce(m[:, t, :], by_expert(lg[:, t, :]), AX_X, ALU.max))
                            v.tensor_reduce(nM[:, t:t + 1], m[:, t, :], AX_X, ALU.max, negate=True).then_inc(maxed, 1)
                            v.tensor_tensor(by_expert(lg[:, t, :]), by_expert(lg[:, t, :]), m[:, t, :].unsqueeze(2).to_broadcast([P, NX, NS]),
                                            ALU.subtract).then_inc(shifted, 1)
                        if gr is not None:
                            add(gr, u0)
                            add(gr, u0 + 1)
                        if exists(b, NB):
                            v.wait_ge(expd, b + 1)
                            link(v.tensor_reduce(z[:, t, :], by_expert(lg[:, t, :]), AX_X, ALU.add))
                            link(v.reciprocal(rz[:, t, :], z[:, t, :]))
                            link(v.tensor_scalar(rz[:, t, :], rz[:, t, :], PS, None, ALU.mult))
                            wait(v, cwf_r, b - 1)
                            v.tensor_tensor(by_expert(dwf[:, t, :]), by_expert(lg[:, t, :]), rz[:, t, :].unsqueeze(2).to_broadcast([P, NX, NS]),
                                            ALU.mult).then_inc(dwf_r, 1)
                            v.wait_ge(em_r, b + 1)
                            link(v.tensor_tensor(wz[:, t, :], z[:, t, :], em[:, t, :], ALU.mult))
                            link(v.tensor_reduce(Z[:, t:t + 1], wz[:, t, :], AX_X, ALU.add))
                            link(v.reciprocal(Z[:, t:t + 1], Z[:, t:t + 1]))
                            v.tensor_scalar(g[:, t, :], wz[:, t, :], Z[:, t:t + 1], None, ALU.mult).then_inc(g_r, 1)
                            v.wait_ge(dwf_r, b + 1)
                            v.wait_ge(dw_hi, b + 1)
                            v.tensor_tensor(dw[:, (s - 2) % RB, 1, :], dwf[:, t, :], dw[:, (s - 2) % RB, 0, :], ALU.subtract).then_inc(dw_lo, 1)
                            assert link.n == LINKS
                        if gr is not None:
                            add(gr, u0 + 2)
                            add(gr, u0 + 3)
                rounds(v, n, body)

            @block.gpsimd
            def _(pool):
                def body(j):
                    for s in range(RB):
                        b = RB * j + s - 2
                        t = s % 2
                        if exists(b, NB):
                            pool.wait_ge(g_r, b + 1)
                            pool.wait_ge(dwf_r, b + 1)
                            wait(pool, cw_hi, b - 1)
                            pool.tensor_tensor(by_expert(cwf[:, t, :]), by_expert(dwf[:, t, :]), g[:, t, :].unsqueeze(2).to_broadcast([P, NX, NS]),
                                               ALU.mult).then_inc(cwf_r, 1)
                            pool.wait_ge(cwf_r, b + 1)
                            pool.wait_ge(cw_hi, b + 1)
                            wait(pool, stored[t], 16 * (GB * j + s // 2 - 1))
                            pool.tensor_tensor(cst[:, t, K:2 * K], cwf[:, t, :], cst[:, t, 0:K], ALU.subtract).then_inc(cw_lo, 1)
                rounds(pool, n, body)

            @block.tensor
            def _(pe):
                def body(j):
                    for s in range(RB):
                        i = RB * j + s
                        t = s % 2
                        if exists(i - 1, NB):
                            pe.wait_ge(xn_lo, i)
                            wait(pe, hi_back, i - 1)
                            wait(pe, lo_back, i - 1)
                            for half in range(2):
                                for c in range(DC):
                                    mm = nc.tensor.transpose(ps_t[:, half, c * P:(c + 1) * P], xn[:, (s - 1) % RB, half, c * P:(c + 1) * P], ident16[:, :])
                            mm.then_inc(turned, 1)
                        b = i - 2
                        if exists(b, NB):
                            pe.wait_ge(hi_back, b + 1)
                            pe.wait_ge(lo_back, b + 1)
                            wait(pe, scaled, b - 1)
                            for c in range(DC):
                                for half, ph in ((0, phi_h), (0, phi_l), (1, phi_h)):
                                    for a in (0, 512):
                                        mm = nc.tensor.matmul(ps_l[:, t, a:a + 512], xT[:, t, half, c * P:(c + 1) * P], ph[:, c, a:a + 512],
                                                              start=(c == 0 and half == 0 and ph is phi_h), stop=(c == DC - 1 and half == 1))
                            mm.then_inc(logits, 1)
                        gr, u0 = group_of(j, s)
                        if gr is not None:
                            first = 0 if s >= GB else GB
                            for u in range(u0, u0 + 4):
                                c, a = u // 2, 512 * (u % 2)
                                pe.wait_ge(dw_lo, GB * (gr + 1))
                                wait(pe, added, NT * gr + u - 1)
                                for q in range(first, first + GB):
                                    for xh, dh in ((0, 0), (0, 1), (1, 0)):
                                        mm = nc.tensor.matmul(ps_s[:, u % 2, :], xn[:, q, xh, c * P:(c + 1) * P], dw[:, q, dh, a:a + 512],
                                                              start=(q == first and xh == 0 and dh == 0), stop=(q == first + GB - 1 and xh == 1))
                                mm.then_inc(tiles, 1)
                rounds(pe, n, body)


def experts(nc, w1, eb1, w2, eb2, slots, eo, ident32):
    with ExitStack() as ctx:
        sems = phase_semaphores(nc, ctx)

        def sem(name):
            sems.append(nc.alloc_semaphore(name))
            return sems[-1]

        def sb(name, shape, dt):
            return ctx.enter_context(nc.sbuf_tensor("e_" + name, shape, dt))

        G = P // NS
        NG = NX // G
        w1s = sb("w1s", [P, 2 * G, DC, H], F32)
        w2s = sb("w2s", [P, G, HC, D], F32)
        bias1 = sb("bias1", [P, 2, H], F32)
        bias2 = sb("bias2", [P, 2, D], F32)
        sl = sb("sl", [P, 2, DC, P], F32)
        hb = sb("hb", [P, 2, H], F32)
        hT = sb("hT", [P, H], F32)
        ps_h = ctx.enter_context(nc.psum_tensor("e_ph", [P, 2, 512], F32))
        ps_g = ctx.enter_context(nc.psum_tensor("e_pg", [P, 512], F32))
        ps_e = ctx.enter_context(nc.psum_tensor("e_pe", [P, 2, 1024], F32))
        w1_in = [sem(f"w1_in{q}") for q in range(2 * G)]
        w2_in = [sem(f"w2_in{q}") for q in range(G)]
        b1_in = [sem(f"b1_in{q}") for q in range(2)]
        b2_in = [sem(f"b2_in{q}") for q in range(2)]
        sl_r, up, hb_r, act_r, turned, back, down, eo_r, tick = (sem("e_" + n) for n in (
            "sl_r", "up", "hb_r", "act_r", "turned", "back", "down", "eo_r", "tick"))
        n = NG // 2 + 1
        eb1_v = eb1.rearrange("(g j) (o h) -> g j o h", j=G, o=1)
        eb2_v = eb2.rearrange("(g j) (o h) -> g j o h", j=G, o=1)
        w1_v = w1.rearrange("e (c p) h -> p e c h", p=P)
        w2_v = w2.rearrange("e (c p) d -> p e c d", p=P)

        with nc.Block() as block:
            @block.sync
            def _(sp):
                def load_up(i, s):
                    wait(sp, up, i - 1)
                    for q in range(G):
                        sp.dma_start(w1s[:, G * s + q], w1_v[:, bass.ds(i * G + q, 1), :, :].rearrange("p o c h -> p (o c) h")).then_inc(w1_in[G * s + q], 16)

                def body(j):
                    for s in range(2):
                        i = 2 * j + s
                        if exists(i, NG):
                            wait(sp, hb_r, i - 1)
                            for q in range(G):
                                sp.dma_start(bias1[NS * q:NS * (q + 1), s, :], eb1[bass.ds(i * G + q, 1), :].to_broadcast([NS, H])).then_inc(b1_in[s], 16)
                            wait(sp, eo_r, i - 1)
                            for q in range(G):
                                sp.dma_start(bias2[NS * q:NS * (q + 1), s, :], eb2[bass.ds(i * G + q, 1), :].to_broadcast([NS, D])).then_inc(b2_in[s], 16)
                            if isinstance(i, int) and i == 0:
                                load_up(0, 0)
                            if exists(i + 1, NG):
                                load_up(i + 1, 1 - s)
                            wait(sp, down, i)
                            for q in range(G):
                                sp.dma_start(w2s[:, q], w2_v[:, bass.ds(i * G + q, 1), :, :].rearrange("p o c h -> p (o c) h")).then_inc(w2_in[q], 16)
                rounds(sp, n, body, head=2, tail=2)

            @block.scalar
            def _(act):
                def body(j):
                    for s in range(2):
                        i = 2 * j + s
                        if exists(i, NG):
                            wait(act, up, i - 1)
                            act.sem_inc(tick, 1)
                            nc.scalar.activation(sl[:, s], slots[:, :, bass.ds(i * P, P)], ACT.Copy, scale=1.0 / (US * PS)).then_inc(sl_r, 1)
                        if exists(i, NG):
                            act.wait_ge(hb_r, i + 1)
                            nc.scalar.activation(hb[:, s, :], hb[:, s, :], ACT.Gelu).then_inc(act_r, 1)
                        if exists(i - 1, NG):
                            act.wait_ge(turned, i)
                            wait(act, down, i - 1)
                            nc.scalar.activation(hT[:, :], ps_g[:, 0:H], ACT.Copy).then_inc(back, 1)
                rounds(act, n, body, head=2)

            @block.vector
            def _(v):
                def body(j):
                    for s in range(2):
                        i = 2 * j + s
                        if exists(i, NG):
                            v.wait_ge(up, i + 1)
                            v.wait_ge(b1_in[s], 16 * G * (j + 1))
                            wait(v, turned, i - 1)
                            v.tensor_tensor(hb[:, s, :], ps_h[:, s, 0:H], bias1[:, s, :], ALU.add).then_inc(hb_r, 1)
                        if exists(i - 1, NG):
                            v.wait_ge(down, i)
                            v.wait_ge(b2_in[1 - s], 16 * G * (j + s))
                            v.tensor_tensor(eo[:, bass.ds(i - 1, 1), :].rearrange("p o d -> p (o d)"), ps_e[:, 1 - s, 0:D], bias2[:, 1 - s, :],
                                            ALU.add).then_inc(eo_r, 1)
                rounds(v, n, body, head=2)

            @block.tensor
            def _(pe):
                def body(j):
                    for s in range(2):
                        i = 2 * j + s
                        if exists(i, NG):
                            pe.wait_ge(sl_r, i + 1)
                            wait(pe, hb_r, i - 1)
                            for q in range(G):
                                pe.wait_ge(w1_in[G * s + q], 16 * (j + 1))
                            for c in range(DC):
                                for q in range(G):
                                    mm = nc.tensor.matmul(ps_h[NS * q:NS * (q + 1), s, 0:H], sl[:, s, c, NS * q:NS * (q + 1)], w1s[:, G * s + q, c, :],
                                                          start=(c == 0), stop=(c == DC - 1))
                            mm.then_inc(up, 1)
                        if exists(i - 1, NG):
                            pe.wait_ge(act_r, i)
                            wait(pe, back, i - 1)
                            for c in range(HC):
                                mm = nc.tensor.transpose(ps_g[:, c * P:(c + 1) * P], hb[:, 1 - s, c * P:(c + 1) * P], ident32[:, :])
                            mm.then_inc(turned, 1)
                            pe.wait_ge(back, i)
                            wait(pe, eo_r, i - 2)
                            for q in range(G):
                                pe.wait_ge(w2_in[q], 16 * i)
                            for c in range(HC):
                                for a, e in ((0, 512), (512, D)):
                                    for q in range(G):
                                        mm = nc.tensor.matmul(ps_e[NS * q:NS * (q + 1), 1 - s, a:e], hT[:, c * P + NS * q:c * P + NS * (q + 1)], w2s[:, q, c, a:e],
                                                              start=(c == 0), stop=(c == HC - 1))
                            mm.then_inc(down, 1)
                rounds(pe, n, body, head=2)


def combine(nc, eo, cw_dram, x2_dram, ident16, out):
    with ExitStack() as ctx:
        sems = phase_semaphores(nc, ctx)

        def sem(name):
            sems.append(nc.alloc_semaphore(name))
            return sems[-1]

        def sb(name, shape, dt):
            return ctx.enter_context(nc.sbuf_tensor("c_" + name, shape, dt))

        eh = sb("eh", [P, KC, D], F16)
        el = sb("el", [P, KC, D], F16)
        inv = sb("inv", [P, 1], F32)
        mx = sb("mx", [P, 1], F32)
        am = sb("am", [P, 1], F32)
        pw = sb("pw", [P, 1], F32)
        sc = sb("sc", [P, 1], F32)
        cw = sb("cw", [P, 2, 2 * K], F16)
        cT = sb("cT", [P, 2, 2, K], F16)
        xb = sb("xb", [P, 2, D], F32)
        ob = sb("ob", [P, 2, D], F32)
        ps_t = ctx.enter_context(nc.psum_tensor("c_pt", [P, 2, 2, 1024], F16))
        ps_o = ctx.enter_context(nc.psum_tensor("c_po", [P, 2, 1024], F32))
        maxed, allmax, scaled, e_hi, e_lo, dve, turned, hi_back, lo_back, prod, summed = (sem("c_" + n) for n in (
            "maxed", "allmax", "scaled", "e_hi", "e_lo", "dve", "turned", "hi_back", "lo_back", "prod", "summed"))
        cw_in = [sem("c_cw0"), sem("c_cw1")]
        x_in = [sem("c_x0"), sem("c_x1")]
        stored = [sem("c_st0"), sem("c_st1")]
        n = (NBR + 1) // 2
        with nc.Block() as block:
            @block.sync
            def _(sp):
                def body(j):
                    for s in range(2):
                        i = 2 * j + s
                        if exists(i, NBR):
                            wait(sp, turned, i - 1)
                            sp.dma_start(cw[:, s, :], cw_dram[bass.ds(i * P, P), :]).then_inc(cw_in[s], 16)
                            wait(sp, summed, i - 1)
                            sp.dma_start(xb[:, s, :], x2_dram[bass.ds(i * P, P), :]).then_inc(x_in[s], 16)
                        b = i - 2
                        if exists(b, NBR):
                            sp.wait_ge(summed, b + 1)
                            rows = TAIL if isinstance(b, int) and b == NBR - 1 else P
                            sp.dma_start(out[bass.ds(b * P, rows), :], ob[0:rows, s, :]).then_inc(stored[s], 16)
                rounds(sp, n + 1, body, head=2, tail=2)
                sp.wait_ge(stored[0], 16 * n)
                sp.wait_ge(stored[1], 16 * (NBR - n))

            @block.gpsimd
            def _(pool):
                pool.wait_ge(maxed, 1)
                pool.partition_all_reduce(am[:, :], mx[:, :], P, bass.bass_isa.ReduceOp.max).then_inc(allmax, 1)

            @block.scalar
            def _(act):
                act.wait_ge(scaled, 1)
                nc.scalar.activation(eh[:, :, :], eo[:, :, :], ACT.Copy, scale=sc[:, 0:1]).then_inc(e_hi, 1)

                def body(j):
                    for s in range(2):
                        i = 2 * j + s
                        if exists(i, NBR):
                            act.wait_ge(turned, i + 1)
                            wait(act, prod, i - 1)
                            nc.scalar.activation(cT[:, s, 0, :], ps_t[:, s, 0, :], ACT.Copy).then_inc(hi_back, 1)
                rounds(act, n, body, head=2)

            @block.vector
            def _(v):
                link = Chain(v, dve)
                v.tensor_reduce(mx[:, :], eo[:, :, :].rearrange("p c d -> p (c d)"), AX_X, ALU.max, apply_absolute_value=True).then_inc(maxed, 1)
                v.wait_ge(allmax, 1)
                power_scale(nc, v, link, am[:, :], pw[:, :], sc[:, :], inv[:, :], TOP)
                v.nop().then_inc(scaled, 1)
                link(v.tensor_scalar(inv[:, :], inv[:, :], 1.0 / PS, None, ALU.mult))
                v.wait_ge(e_hi, 1)
                v.scalar_tensor_tensor(el[:, :, :].rearrange("p c d -> p (c d)"), eo[:, :, :].rearrange("p c d -> p (c d)"), sc[:, 0:1],
                                       eh[:, :, :].rearrange("p c d -> p (c d)"), ALU.mult, ALU.subtract).then_inc(e_lo, 1)

                def body(j):
                    for s in range(2):
                        i = 2 * j + s
                        if exists(i, NBR):
                            v.wait_ge(turned, i + 1)
                            wait(v, prod, i - 1)
                            v.tensor_copy(cT[:, s, 1, :], ps_t[:, s, 1, :]).then_inc(lo_back, 1)
                        b = i - 1
                        if exists(b, NBR):
                            v.wait_ge(prod, b + 1)
                            v.wait_ge(x_in[1 - s], 16 * (j + s))
                            wait(v, stored[1 - s], 16 * (j + s - 1))
                            v.scalar_tensor_tensor(ob[:, 1 - s, :], ps_o[:, 1 - s, 0:D], inv[:, 0:1], xb[:, 1 - s, :], ALU.mult, ALU.add).then_inc(summed, 1)
                rounds(v, n, body, head=2)

            @block.tensor
            def _(pe):
                def body(j):
                    for s in range(2):
                        i = 2 * j + s
                        if exists(i, NBR):
                            pe.wait_ge(cw_in[s], 16 * (j + 1))
                            wait(pe, hi_back, i - 1)
                            wait(pe, lo_back, i - 1)
                            for half in range(2):
                                for c in range(KC):
                                    mm = nc.tensor.transpose(ps_t[:, s, half, c * P:(c + 1) * P], cw[:, s, half * K + c * P:half * K + (c + 1) * P], ident16[:, :])
                            mm.then_inc(turned, 1)
                        b = i - 1
                        if exists(b, NBR):
                            pe.wait_ge(hi_back, b + 1)
                            pe.wait_ge(lo_back, b + 1)
                            pe.wait_ge(e_lo, 1)
                            wait(pe, summed, b - 1)
                            for c in range(KC):
                                for half, ee in ((0, eh), (0, el), (1, eh)):
                                    for a, e in ((0, 512), (512, D)):
                                        mm = nc.tensor.matmul(ps_o[:, 1 - s, a:e], cT[:, 1 - s, half, c * P:(c + 1) * P], ee[:, c, a:e],
                                                              start=(c == 0 and half == 0 and ee is eh), stop=(c == KC - 1 and half == 1))
                            mm.then_inc(prod, 1)
                rounds(pe, n, body, head=2)


_INS = ["x", "src", "dst", "L0_gnn_W1", "L0_gnn_b1", "L0_gnn_W2", "L0_gnn_b2", "L0_ffn_phi", "L0_ffn_scale",
        "L0_ffn_w1", "L0_ffn_b1", "L0_ffn_w2", "L0_ffn_b2"]


def kernel(**inputs):
    import numpy as _np
    import concourse.bacc as _bacc
    from concourse import mybir as _mybir
    from concourse.bass_utils import run_bass_kernel_spmd as _run

    nc = _bacc.Bacc("TRN2", target_bir_lowering=False, num_devices=1)
    arrays, args = {}, []
    for name in _INS:
        a = _np.ascontiguousarray(inputs[name])
        arrays[f"in_{name}_dram"] = a
        args.append(nc.dram_tensor(f"in_{name}_dram", a.shape, _mybir.dt.from_np(a.dtype), kind="ExternalInput").ap())
    out = nc.dram_tensor("out_0_dram", (N, D), F32, kind="ExternalOutput").ap()
    gnn_ffn(nc, *args, out)
    r = _run(nc, [arrays], core_ids=[0])
    return r.results[0]["out_0_dram"]
```

```python
from contextlib import ExitStack

import concourse.bass as bass
from concourse import mybir

F32 = mybir.dt.float32
F16 = mybir.dt.float16
I32 = mybir.dt.int32
ALU = mybir.AluOpType
ACT = mybir.ActivationFunctionType
AX_X = mybir.AxisListType.X

P = 128
N = 6250
D = 768
E = 100000
DC = D // P
NBR = (N + P - 1) // P
NB = 50
TAIL = N - (NBR - 1) * P
ET = (E + P - 1) // P
EF = E // P
QC = 7
QS = 4
NSTEP = 440
QUAD = 4
RING = 2 * QUAD
AR = 8
CREDIT = 1
FIRST = QUAD + 2
NQ = NSTEP // QUAD
NEV = NQ + NBR
IW = 20
HT = 8
NX = 32
NS = 32
K = NX * NS
H = 384
HC = H // P
KC = K // P
GB = 2
EPS_LN = 1e-5
EPS_L2 = 1e-12
XS = 2.0 ** 10
AS = 2.0 ** -8
US = 2.0 ** 10
PS = 2.0 ** 14
TOP = 2.0 ** 14
assert (ET + 1) // 2 + NBR - 1 <= NSTEP <= QS * P and ET <= QC * P and NSTEP % (2 * IW) == 0 and NEV <= 160


def wait(eng, sem, value):
    if isinstance(value, int) and value <= 0:
        return
    eng.wait_ge(sem, value)


def rounds(eng, n, body, head=1, tail=1):
    for i in range(head):
        body(i)
    with eng.Fori(head, n - tail) as i:
        body(i)
    for i in range(n - tail, n):
        body(i)


def phase_semaphores(nc, ctx):
    sems = []

    def clear():
        nc.clear_and_free_semaphores(sems)
        nc.all_engine_barrier()
    ctx.callback(clear)
    return sems


def exists(b, n):
    return not isinstance(b, int) or 0 <= b < n


class Chain:

    def __init__(self, eng, sem):
        self.eng, self.sem, self.n, self.base = eng, sem, 0, 0

    def at(self, base):
        self.base, self.n = base, 0

    def __call__(self, ins):
        self.n += 1
        ins.then_inc(self.sem, 1)
        self.eng.wait_ge(self.sem, self.base + self.n)


def gnn_ffn(nc, x, src, dst, W1, b1, W2, b2, phi, scale, w1, eb1, w2, eb2, out):
    src_pad = nc.dram_tensor("src_pad", (QC * P, P), I32).ap()
    dst_pad = nc.dram_tensor("dst_pad", (QC * P, P), I32).ap()
    blk_dram = nc.dram_tensor("blk_dram", (QS, P), I32).ap()
    table1 = nc.dram_tensor("table1", (NBR * P, 2 * D), F16).ap()
    table2 = nc.dram_tensor("table2", (NBR * P, 2 * D), F16).ap()
    x2_dram = nc.dram_tensor("x2_dram", (NB * P, D), F32).ap()
    cw_dram = nc.dram_tensor("cw_dram", (NB * P, 2 * K), F16).ap()

    idx_dram = nc.dram_tensor("idx_dram", (P, 2 * NSTEP), I32).ap()
    h_dram = nc.dram_tensor("h_dram", (NBR * P, D), F32).ap()
    ev_dram = nc.dram_tensor("ev_dram", (2, 2, P), I32).ap()

    with ExitStack() as top:
        ident16 = top.enter_context(nc.sbuf_tensor("ident16", [P, P], F16))
        valid = top.enter_context(nc.sbuf_tensor("valid", [P, NB], F32))
        mv2 = top.enter_context(nc.sbuf_tensor("mv2", [P, NB, 2], F32))
        with ExitStack() as gnn:
            def sb(name, shape, dt):
                return gnn.enter_context(nc.sbuf_tensor(name, shape, dt))

            iota_j = sb("iota_j", [P, P], F16)
            dloc = sb("dloc", [P, 2, NSTEP + QUAD], F32)
            blk = sb("blk", [1, NQ], I32)
            ev = sb("ev", [1, 40], I32)
            dinv = sb("dinv", [P, NBR], F32)
            dinv_as = sb("dinv_as", [P, NBR], F32)
            dinv_s2 = sb("dinv_s2", [P, NBR], F32)
            back = sb("back", [P, 1], F32)
            lnf = sb("lnf", [P, NBR], F32)
            lnb = sb("lnb", [P, NBR], F32)
            with ExitStack() as early:
                acc = early.enter_context(nc.sbuf_tensor("xs", [P, NBR, D], F32))
                prepare(nc, x, src, dst, src_pad, dst_pad, blk_dram, idx_dram, ev_dram, acc, dloc, blk, ev, dinv, dinv_as,
                        lnf, lnb, mv2, valid, ident16, iota_j)
                first_table(nc, acc, lnf, lnb, table1)
            for layer, W, bias, table in ((1, W1, b1, table1), (2, W2, b2, table2)):
                convolve(nc, layer, W, bias, table, idx_dram, dloc, blk, ev, dinv, dinv_as, dinv_s2, lnf, lnb, back, mv2,
                         ident16, iota_j, table2, x, h_dram, x2_dram)
        with ExitStack() as ffn:
            slots = ffn.enter_context(nc.sbuf_tensor("slots", [P, DC, K], F32))
            dispatch(nc, phi, scale, x2_dram, cw_dram, slots, mv2, valid, ident16)
            with ExitStack() as late:
                eo = late.enter_context(nc.sbuf_tensor("eo", [P, KC, D], F32))
                experts(nc, w1, eb1, w2, eb2, slots, eo, ident16)
                combine(nc, eo, cw_dram, x2_dram, ident16, out)


def prepare(nc, x, src, dst, src_pad, dst_pad, blk_dram, idx_dram, ev_dram, acc, dloc, blk, ev, dinv, dinv_as,
            lnf, lnb, mv2, valid, ident16, iota_j):
    with ExitStack() as ctx:
        sems = phase_semaphores(nc, ctx)

        def sem(name):
            sems.append(nc.alloc_semaphore(name))
            return sems[-1]

        def sb(name, shape, dt):
            return ctx.enter_context(nc.sbuf_tensor(name, shape, dt))

        def ps(name, shape, dt):
            return ctx.enter_context(nc.psum_tensor(name, shape, dt))

        raw_src = sb("raw_src", [P, 2 * QS, P], I32)
        raw_dst = sb("raw_dst", [P, 2 * QS, P], I32)
        work = sb("work", [P, 2 * QS, P], F32)
        work2 = sb("work2", [P, 2 * QS, P], F32)
        ident32 = sb("ident32", [P, P], F32)
        ones32 = sb("ones32", [P, P], F32)
        total = sb("total", [P, NBR], F32)
        nmean = sb("nmean", [P, NBR], F32)
        squares = sb("squares", [P, NBR], F32)
        idx = sb("idx", [P, QS * P, 2], I32)
        ev_e = sb("ev_e", [P, 2], F32)
        ev_at = sb("ev_at", [P, NBR], F32)
        ev_ati = sb("ev_ati", [P, NBR], I32)
        ev_past = sb("ev_past", [P, 2, NBR], F32)
        ev_c = sb("ev_c", [P, 2, 2], F32)
        ev_i = sb("ev_i", [P, 2, 2], I32)
        ev_row = sb("ev_row", [1, 2, 2, P], I32)
        ev_f = sb("ev_f", [1, 4, 40], F32)
        b_one = sb("b_one", [P, NBR], F32)
        ev_m = sb("ev_m", [1, 40], F32)
        pair_src, pair_dst, fsrc, fdst = (a[:, :, :].rearrange("p (q h) e -> p q (h e)", h=2) for a in (raw_src, raw_dst, work, work2))
        lo16 = sb("lo16", [P, QC * P], F16)
        hi16 = sb("hi16", [P, QC * P], F16)
        iota_b = sb("iota_b", [P, NBR], F16)
        oh_lo = sb("oh_lo", [P, 2, HT, P], F16)
        oh_hi = sb("oh_hi", [P, 2, HT, NBR], F16)
        ones16 = sb("ones16", [P, P], F16)
        zeros16 = sb("zeros16", [P, P], F16)
        diff = sb("diff", [P, P], F32)
        node = sb("node", [P, NB], F32)
        step_k = sb("step_k", [P, QS], F32)
        blk_row = sb("blk_row", [1, QS * P], I32)
        blk_w = sb("blk_w", [1, QS * P // 4], F32)

        b_num = sb("b_num", [P, NBR - 1], F32)
        deg = sb("deg", [P, NBR], F32)
        cnt = sb("cnt", [P, NBR], F32)
        ones_b = sb("ones_b", [P, NBR], F32)
        cum = sb("cum", [P, NBR], F32)
        cum_i = sb("cum_i", [P, NBR], I32)
        thr = sb("thr", [P, NBR - 1], F32)
        past = sb("past", [P, QS, NBR - 1], F32)
        bk = sb("bk", [P, QS], F32)
        bk128 = sb("bk128", [P, QS], F32)
        tk = sb("tk", [P, QS], F32)
        tk_i = sb("tk_i", [P, QS], I32)
        bk_i = sb("bk_i", [P, QS], I32)
        rstd = sb("rstd", [P, NBR], F32)
        psT = ps("psT", [P, 1024], F32)
        psU = ps("psU", [P, 1024], F32)
        psD = ps("psD", [P, 512], F32)
        psC = ps("psC", [P, 512], F32)
        unused = sb("unused", [P, 2, D], F16)

        iotas = sem("iotas")
        consts = sem("consts")
        fills = sem("fills")
        edges_in = sem("edges_in")
        edges_out = sem("edges_out")
        x_in = sem("x_in")
        dst_f = sem("dst_f")
        dst_t = sem("dst_t")
        codes = sem("codes")
        lo_ready = sem("lo_ready")
        hi_ready = sem("hi_ready")
        oh_used = sem("oh_used")
        deg_done = sem("deg_done")
        dve = sem("prep_dve")
        deg_read = sem("deg_read")
        rooted = sem("rooted")
        cnt_sum = sem("cnt_sum")
        steps_ready = sem("steps_ready")
        tiles_in = sem("tiles_in")
        tiles_f = sem("tiles_f")
        tiles_t = sem("tiles_t")
        blk_out = sem("blk_out")
        blk_in = sem("blk_in")
        evs_ready = sem("evs_ready")
        ev_out = sem("ev_out")
        ev_in = sem("ev_in")
        idx_ready = sem("idx_ready")
        idx_out = sem("idx_out")
        totals = sem("totals")
        means = sem("means")
        tick = sem("prep_tick")
        sq_ready = sem("sq_ready")
        var_ready = sem("var_ready")
        std_ready = sem("std_ready")
        nround = (ET + 2 * HT - 1) // (2 * HT)

        with nc.Block() as block:
            @block.sync
            def _(sp):
                sp.wait_ge(fills, 2)
                full = (QC - 1) * P * P
                for raw, e in ((raw_dst, dst), (raw_src, src)):
                    sp.dma_start(raw[:, 0:QC - 1, :], e[0:full].rearrange("(q p e) -> p q e", p=P, e=P)).then_inc(edges_in, 16)
                    rest = EF - (QC - 1) * P
                    sp.dma_start(raw[0:rest, QC - 1, :], e[full:EF * P].rearrange("(p e) -> p e", e=P)).then_inc(edges_in, 16)
                    sp.dma_start(raw[rest:rest + 1, QC - 1, 0:E - EF * P], e[EF * P:E].rearrange("(p e) -> p e", p=1)).then_inc(edges_in, 16)
                sp.wait_ge(edges_in, 96)
                sp.dma_start(dst_pad.rearrange("(q p) e -> p q e", p=P), raw_dst[:, 0:QC, :]).then_inc(edges_out, 16)
                sp.dma_start(src_pad.rearrange("(q p) e -> p q e", p=P), raw_src[:, 0:QC, :]).then_inc(edges_out, 16)
                sp.wait_ge(fills, 3)
                for c in range(0, NBR - 1, 8):
                    sp.dma_start(acc[:, c:c + 8, :], x[c * P:(c + 8) * P, :].rearrange("(b p) d -> p b d", p=P)).then_inc(x_in, 16)
                sp.dma_start(acc[0:TAIL, NBR - 1, :], x[(NBR - 1) * P:N, :]).then_inc(x_in, 16)
                sp.wait_ge(steps_ready, 1)
                sp.dma_start(blk_dram.rearrange("q p -> p q"), bk_i[:, :], allow_slow_non_contiguous=True).then_inc(blk_out, 16)
                sp.wait_ge(blk_out, 16)
                sp.dma_start(blk_row[:, :], blk_dram.rearrange("(o q) p -> o (q p)", o=1)).then_inc(blk_in, 16)
                sp.wait_ge(evs_ready, 1)
                sp.dma_start(ev_dram.rearrange("a c p -> p a c"), ev_i[:, :, :], allow_slow_non_contiguous=True).then_inc(ev_out, 16)
                sp.wait_ge(ev_out, 16)
                sp.dma_start(ev_row[:, :, :, :], ev_dram.rearrange("(o a) c p -> o a c p", o=1)).then_inc(ev_in, 16)
                sp.wait_ge(idx_ready, 1)
                sp.dma_start(idx_dram, idx[:, 0:NSTEP, :].rearrange("p k h -> p (k h)")).then_inc(idx_out, 16)
                sp.wait_ge(blk_in, 16)
                sp.wait_ge(ev_in, 16)
                sp.wait_ge(idx_out, 16)
                sp.wait_ge(edges_out, 32)

            @block.gpsimd
            def _(pool):
                pool.iota(iota_j[:, :], [[1, P]], base=0, channel_multiplier=0, allow_small_or_imprecise_dtypes=True).then_inc(iotas, 1)
                pool.iota(iota_b[:, :], [[1, NBR]], base=0, channel_multiplier=0, allow_small_or_imprecise_dtypes=True).then_inc(iotas, 1)
                pool.iota(diff[:, :], [[1, P]], base=0, channel_multiplier=-1, allow_small_or_imprecise_dtypes=True).then_inc(iotas, 1)
                pool.iota(node[:, :], [[P, NB]], base=0, channel_multiplier=1, allow_small_or_imprecise_dtypes=True).then_inc(iotas, 1)
                pool.iota(step_k[:, :], [[P, QS]], base=0, channel_multiplier=1, allow_small_or_imprecise_dtypes=True).then_inc(iotas, 1)
                pool.iota(b_num[:, :], [[1, NBR - 1]], base=1, channel_multiplier=0, allow_small_or_imprecise_dtypes=True).then_inc(iotas, 1)
                pool.iota(ev_e[:, :], [[P, 2]], base=0, channel_multiplier=1, allow_small_or_imprecise_dtypes=True).then_inc(iotas, 1)
                pool.iota(b_one[:, :], [[1, NBR]], base=1, channel_multiplier=0, allow_small_or_imprecise_dtypes=True).then_inc(iotas, 1)
                pool.iota(ev_m[:, :], [[4, 40]], base=0, channel_multiplier=0, allow_small_or_imprecise_dtypes=True).then_inc(iotas, 1)
                pool.wait_ge(iotas, 9)
                pool.wait_ge(steps_ready, 2)
                pool.wait_ge(dst_f, 1)
                pool.wait_ge(edges_out, 32)
                for q in range(QS):
                    for pair, pad in ((pair_src, src_pad), (pair_dst, dst_pad)):
                        pool.indirect_dma_start(out=pair[:, q, :], out_offset=None, in_=pad.rearrange("(t h) e -> t (h e)", h=2),
                                                in_offset=bass.IndirectOffsetOnAxis(ap=tk_i[:, q:q + 1], axis=0)).then_inc(tiles_in, 16)

            @block.scalar
            def _(act):
                act.wait_ge(x_in, 16 * 7)

                def pass_over(done, func, result):
                    def body(i):
                        for q in range(7):
                            b = 7 * i + q
                            wait(act, done, b if q == 0 else b - 1)
                            act.sem_inc(tick, 1)
                            offset = {"bias": nmean[:, bass.ds(b, 1)]} if func == ACT.Square else {}
                            nc.scalar.activation(unused[:, q % 2, 0:D], acc[:, bass.ds(b, 1), :].rearrange("p o d -> p (o d)"), func,
                                                 accum_out=result[:, bass.ds(b, 1)], **offset).then_inc(done, 1)
                    rounds(act, NBR // 7, body)
                pass_over(totals, ACT.Copy, total)
                act.wait_ge(totals, NBR)
                nc.scalar.activation(nmean[:, :], total[:, :], ACT.Copy, scale=-1.0 / D).then_inc(means, 1)
                act.wait_ge(means, 1)
                act.sem_inc(tick, 1)
                pass_over(sq_ready, ACT.Square, squares)
                act.wait_ge(deg_read, 1)
                nc.scalar.activation(dinv[:, 0:NBR], deg[:, 0:NBR], ACT.Sqrt).then_inc(rooted, 1)
                act.wait_ge(var_ready, 1)
                nc.scalar.activation(rstd[:, :], rstd[:, :], ACT.Sqrt).then_inc(std_ready, 1)

            @block.tensor
            def _(pe):
                pe.wait_ge(consts, 5)
                pe.wait_ge(dst_f, 1)
                for q in range(QC):
                    mm = nc.tensor.transpose(psT[:, q * P:(q + 1) * P], work[:, q, :], ident32[:, :])
                mm.then_inc(dst_t, 1)
                nc.tensor.matmul(psD[:, 0:NBR], ident16[:, :], ones16[:, 0:NBR], start=True, stop=False, skip_group_check=True)

                def count(i):
                    for s in range(2):
                        c = 2 * i + s
                        pe.wait_ge(lo_ready, c + 1)
                        pe.wait_ge(hi_ready, c + 1)
                        for t in range(HT):
                            mm = nc.tensor.matmul(psD[:, 0:NBR], oh_lo[:, s, t, :], oh_hi[:, s, t, :], start=False, stop=False, skip_group_check=True)
                        mm.then_inc(oh_used, 1)
                rounds(pe, nround, count)
                nc.tensor.matmul(psD[:, 0:NBR], zeros16[:, :], ones16[:, 0:NBR], start=False, stop=True, skip_group_check=True).then_inc(deg_done, 1)
                pe.wait_ge(deg_read, 2)
                nc.tensor.matmul(psC[:, 0:NBR], ones32[:, :], cnt[:, :], start=True, stop=True).then_inc(cnt_sum, 1)
                pe.wait_ge(tiles_f, 2)
                for h in range(2):
                    for q in range(QS):
                        to = h * QS * P + q * P
                        nc.tensor.transpose(psT[:, to:to + P], fdst[:, q, h * P:(h + 1) * P], ident32[:, :])
                        mm = nc.tensor.transpose(psU[:, to:to + P], fsrc[:, q, h * P:(h + 1) * P], ident32[:, :])
                mm.then_inc(tiles_t, 1)

            @block.vector
            def _(v):
                link = Chain(v, dve)
                v.memset(raw_dst[:, QC - 1, :], -1).then_inc(fills, 1)
                v.memset(raw_src[:, QC - 1, :], 0).then_inc(fills, 1)
                v.memset(acc[:, NBR - 1:NBR, :], 0.0).then_inc(fills, 1)
                v.memset(mv2[:, NBR:NB, :], 0.0)
                v.memset(ones16[:, :], 1.0).then_inc(consts, 1)
                v.memset(zeros16[:, :], 0.0).then_inc(consts, 1)
                v.memset(ones32[:, :], 1.0).then_inc(consts, 1)
                v.memset(ones_b[:, :], 1.0)
                v.wait_ge(iotas, 9)
                v.tensor_scalar(ident16[:, :], diff[:, :], 0.0, None, ALU.is_equal).then_inc(consts, 1)
                v.tensor_scalar(ident32[:, :], diff[:, :], 0.0, None, ALU.is_equal).then_inc(consts, 1)
                v.tensor_scalar(valid[:, :], node[:, :], float(N), None, ALU.is_lt)
                v.wait_ge(edges_in, 96)
                v.tensor_copy(work[:, 0:QC, :], raw_dst[:, 0:QC, :]).then_inc(dst_f, 1)
                v.wait_ge(dst_t, 1)
                link(v.tensor_copy(as_int(work), psT[:, 0:QC * P]))
                wi = as_int(work)
                w2i = as_int(work2)
                link(v.tensor_scalar(w2i, wi, 127, None, ALU.bitwise_and))
                v.tensor_copy(lo16[:, :], w2i).then_inc(codes, 1)
                v.wait_ge(codes, 1)
                link(v.tensor_scalar(w2i, wi, 7, None, ALU.arith_shift_right))
                v.tensor_copy(hi16[:, :], w2i).then_inc(codes, 1)
                v.wait_ge(codes, 2)

                def hot_nodes(i):
                    for s in range(2):
                        c = 2 * i + s
                        wait(v, oh_used, c - 1)
                        v.tensor_tensor(
                            oh_lo[:, s], iota_j[:, :].unsqueeze(1).to_broadcast([P, HT, P]),
                            lo16[:, bass.ds(c * HT, HT)].unsqueeze(2).to_broadcast([P, HT, P]), ALU.is_equal).then_inc(lo_ready, 1)
                        v.tensor_tensor(
                            oh_hi[:, s], iota_b[:, :].unsqueeze(1).to_broadcast([P, HT, NBR]),
                            hi16[:, bass.ds(c * HT, HT)].unsqueeze(2).to_broadcast([P, HT, NBR]), ALU.is_equal).then_inc(hi_ready, 1)
                rounds(v, nround, hot_nodes)
                v.wait_ge(deg_done, 1)
                v.tensor_copy(deg[:, 0:NBR], psD[:, 0:NBR]).then_inc(deg_read, 1)
                v.wait_ge(deg_read, 1)
                v.tensor_scalar(cnt[:, :], deg[:, 0:NBR], -1.0, None, ALU.add).then_inc(deg_read, 1)
                v.wait_ge(sq_ready, NBR)
                v.tensor_scalar(rstd[:, :], squares[:, :], 1.0 / D, EPS_LN, ALU.mult, ALU.add).then_inc(var_ready, 1)
                v.wait_ge(rooted, 1)
                link(v.reciprocal(dinv[:, 0:NBR], dinv[:, 0:NBR]))
                v.tensor_scalar(dinv_as[:, :], dinv[:, :], AS, None, ALU.mult)
                v.wait_ge(std_ready, 1)
                link(v.reciprocal(rstd[:, :], rstd[:, :]))
                link(v.scalar_tensor_tensor(lnf[:, :], rstd[:, :], XS, dinv[:, :], ALU.mult, ALU.mult))
                v.tensor_tensor(lnb[:, :], nmean[:, :], lnf[:, :], ALU.mult)
                v.wait_ge(cnt_sum, 1)
                link(v.tensor_tensor_scan(cum[:, :], ones_b[:, :], psC[:, 0:NBR], 0.0, ALU.mult, ALU.add))
                link(v.tensor_copy(cum_i[:, :], cum[:, :]))
                link(v.tensor_scalar(cum_i[:, :], cum_i[:, :], 8, None, ALU.arith_shift_right))
                link(v.tensor_copy(cum[:, :], cum_i[:, :]))
                link(v.tensor_tensor(thr[:, :], cum[:, 0:NBR - 1], b_num[:, :], ALU.add))
                link(v.tensor_tensor(past[:, :, :], step_k[:, :].unsqueeze(2).to_broadcast([P, QS, NBR - 1]),
                                     thr[:, :].unsqueeze(1).to_broadcast([P, QS, NBR - 1]), ALU.is_ge))
                link(v.tensor_reduce(bk[:, :], past[:, :, :], AX_X, ALU.add))
                v.tensor_copy(bk_i[:, :], bk[:, :]).then_inc(steps_ready, 1)
                link(v.tensor_scalar(bk128[:, :], bk[:, :], float(P), None, ALU.mult))
                link(v.tensor_tensor(tk[:, :], step_k[:, :], bk[:, :], ALU.subtract))
                link(v.tensor_scalar(tk[:, :], tk[:, :], float(QC * P // 2 - 1), None, ALU.min))
                v.wait_ge(steps_ready, 1)
                v.tensor_copy(tk_i[:, :], tk[:, :]).then_inc(steps_ready, 1)
                link(v.tensor_scalar(ev_at[:, 0:NBR - 1], thr[:, :], -1.0, None, ALU.add))
                link(v.memset(ev_at[:, NBR - 1:NBR], float(NSTEP - 1)))
                link(v.tensor_copy(ev_ati[:, :], ev_at[:, :]))
                link(v.tensor_scalar(ev_ati[:, :], ev_ati[:, :], 2, None, ALU.arith_shift_right))
                link(v.tensor_copy(ev_at[:, :], ev_ati[:, :]))
                link(v.tensor_tensor(ev_at[:, :], ev_at[:, :], b_one[:, :], ALU.add))
                for c, op in ((0, ALU.is_gt), (1, ALU.is_equal)):
                    link(v.tensor_tensor(ev_past[:, :, :], ev_e[:, :].unsqueeze(2).to_broadcast([P, 2, NBR]),
                                         ev_at[:, :].unsqueeze(1).to_broadcast([P, 2, NBR]), op))
                    link(v.tensor_reduce(ev_c[:, :, c], ev_past[:, :, :], AX_X, ALU.add))
                v.tensor_copy(ev_i[:, :, :], ev_c[:, :, :]).then_inc(evs_ready, 1)
                v.wait_ge(tiles_in, 16 * 2 * QS)
                for q in range(QS):
                    last = v.tensor_scalar(fdst[:, q, :], pair_dst[:, q, :], bk128[:, q:q + 1], None, ALU.subtract)
                last.then_inc(tiles_f, 1)
                v.tensor_copy(fsrc[:, :, :], pair_src[:, :, :]).then_inc(tiles_f, 1)
                v.wait_ge(blk_in, 16)
                four = blk_row[:, :].rearrange("o (m r) -> o m r", r=4)
                link(v.tensor_copy(blk_w[:, :], four[:, :, 0]))
                for r in range(1, 4):
                    link(v.scalar_tensor_tensor(blk_w[:, :], four[:, :, r], float(64 ** r), blk_w[:, :], ALU.mult, ALU.add))
                v.tensor_copy(blk[:, :], blk_w[:, 0:NQ])
                v.wait_ge(ev_in, 16)
                for a, z in ((0, 32), (32, 40)):
                    q = a // 32
                    def of(c, r):
                        return ev_row[:, q, c, :].rearrange("o (m r) -> o m r", r=4)[:, 0:z - a, r]
                    w, vb, t2 = ev_f[:, 0, a:z], ev_f[:, 1, a:z], ev_f[:, 2, a:z]
                    link(v.tensor_copy(vb, of(1, 0)))
                    for r in range(1, 4):
                        link(v.scalar_tensor_tensor(vb, of(1, r), float(2 ** r), vb, ALU.mult, ALU.add))
                    link(v.tensor_scalar(w, vb, -15.0, 15.0 * 16.0, ALU.mult, ALU.add))
                    link(v.scalar_tensor_tensor(t2, of(0, 0), -1.0, ev_m[:, a:z], ALU.mult, ALU.add))
                    link(v.scalar_tensor_tensor(w, t2, 256.0, w, ALU.mult, ALU.add))
                    link(v.scalar_tensor_tensor(w, of(0, 0), 32768.0, w, ALU.mult, ALU.add))
                v.tensor_copy(ev[:, :], ev_f[:, 0, :])
                v.wait_ge(tiles_t, 1)
                v.tensor_copy(dloc[:, :, :], psT[:, 0:2 * QS * P].rearrange("p (h k) -> p h k", h=2)[:, :, 0:NSTEP + QUAD])
                v.tensor_copy(idx[:, :, :].rearrange("p k h -> p h k"), psU[:, 0:2 * QS * P].rearrange("p (h k) -> p h k", h=2)).then_inc(idx_ready, 1)


def as_int(work):
    return work[:, 0:QC, :].rearrange("p q e -> p (q e)").bitcast(I32)


def first_table(nc, acc, lnf, lnb, table):
    with ExitStack() as ctx:
        sems = phase_semaphores(nc, ctx)

        def sem(name):
            sems.append(nc.alloc_semaphore(name))
            return sems[-1]

        TR = 7
        stage = ctx.enter_context(nc.sbuf_tensor("stage", [P, TR, 2 * D], F16))
        hi_ready = sem("t1_hi")
        acc_ready = sem("t1_acc")
        lo_ready = sem("t1_lo")
        stored = [sem(f"t1_st{s}") for s in range(TR)]
        tick = sem("t1_tick")
        n = NBR // TR
        with nc.Block() as block:
            @block.scalar
            def _(act):
                def body(i):
                    for s in range(TR):
                        b = TR * i + s
                        wait(act, stored[s], 16 * i)
                        act.sem_inc(tick, 1)
                        f, c = lnf[:, bass.ds(b, 1)], lnb[:, bass.ds(b, 1)]
                        rows = acc[:, bass.ds(b, 1), :].rearrange("p o d -> p (o d)")
                        nc.scalar.activation(stage[:, s, 0:D], rows, ACT.Identity, bias=c, scale=f).then_inc(hi_ready, 1)
                rounds(act, n, body)

            @block.vector
            def _(v):
                def body(i):
                    for s in range(TR):
                        b = TR * i + s
                        v.wait_ge(hi_ready, b + 1)
                        wait(v, stored[s], 16 * i)
                        rows = acc[:, bass.ds(b, 1), :].rearrange("p o d -> p (o d)")
                        v.tensor_scalar(rows, rows, lnf[:, bass.ds(b, 1)], lnb[:, bass.ds(b, 1)], ALU.mult, ALU.add).then_inc(acc_ready, 1)
                        v.wait_ge(acc_ready, b + 1)
                        v.tensor_tensor(stage[:, s, D:2 * D], rows, stage[:, s, 0:D], ALU.subtract).then_inc(lo_ready, 1)
                rounds(v, n, body)

            @block.sync
            def _(sp):
                def body(i):
                    for s in range(TR):
                        b = TR * i + s
                        sp.wait_ge(hi_ready, b + 1)
                        sp.wait_ge(lo_ready, b + 1)
                        sp.dma_start(table[bass.ds(b * P, P), :], stage[:, s, :]).then_inc(stored[s], 16)
                rounds(sp, n, body)
                for s in range(TR):
                    sp.wait_ge(stored[s], 16 * n)


def power_scale(nc, v, link, val, pw, sc, inv, top):
    link(v.tensor_scalar(val, val, 1e-20, None, ALU.max))
    link(v.tensor_scalar(pw.bitcast(I32), val.bitcast(I32), 0x7F800000, None, ALU.bitwise_and))
    link(v.reciprocal(sc, pw))
    link(v.tensor_scalar(sc, sc, top, None, ALU.mult))
    link(v.tensor_scalar(inv, pw, 1.0 / top, None, ALU.mult))


def events(eng, ev, word, n, quad, visit):
    w = eng.value_load(ev[0:1, bass.ds(word, 1)], min_val=0, max_val=(NBR + 1) * 2 ** 15)
    b = eng.snap(w >> 15)
    m = eng.snap((w >> 8) & 127)
    for r in range(n):
        with eng.If(((w >> r) & 1) > 0):
            visit(b.with_bounds(min_val=0, max_val=NBR - 1), m)
        with eng.Else():
            quad(m.with_bounds(min_val=0, max_val=NQ - 1))
        if r < n - 1:
            b = eng.snap(b + ((w >> r) & 1))
            m = eng.snap(m + ((w >> (4 + r)) & 1))


def all_events(eng, ev, quad, visit):
    with eng.Fori(0, NEV // 4) as word:
        events(eng, ev, word, 4, quad, visit)
    if NEV % 4:
        events(eng, ev, NEV // 4, NEV % 4, quad, visit)


def convolve(nc, layer, W, bias, table, idx_dram, dloc, blk, ev, dinv, dinv_as, dinv_s2, lnf, lnb, back, mv2,
             ident16, iota_j, table2, x, h_dram, x2_dram):
    g = f"d{layer}_"
    with ExitStack() as ctx:
        sems = phase_semaphores(nc, ctx)

        def sem(name):
            sems.append(nc.alloc_semaphore(name))
            return sems[-1]

        def sb(name, shape, dt):
            return ctx.enter_context(nc.sbuf_tensor(g + name, shape, dt))

        Wh = sb("Wh", [P, DC, D], F16)
        Wl = sb("Wl", [P, DC, D], F16)
        brow = sb("brow", [P, D], F32)
        inv = sb("inv", [P, 1], F32)
        acc = sb("acc", [P, AR, D], F32)
        zeros = sb("zeros", [P, D], F32)

        def rows_of(b):
            return acc[:, bass.ds(b % AR if isinstance(b, int) else b & (AR - 1), 1), :].rearrange("p o d -> p (o d)")

        def own_rows(b, rows):
            return (x if layer == 1 else h_dram)[bass.ds(b * P, rows), :]

        def normalise(b, count):
            nc.scalar.activation(rows_of(b), rows_of(b), ACT.Identity, bias=lnb[:, bass.ds(b, 1)], scale=lnf[:, bass.ds(b, 1)]).then_inc(count, 1)

        with ExitStack() as pre:
            def sbp(name, shape, dt):
                return pre.enter_context(nc.sbuf_tensor(g + name, shape, dt))
            Wf = sbp("Wf", [P, DC, D], F32)
            mx = sbp("mx", [P, 1], F32)
            bm = sbp("bm", [P, 1], F32)
            wm = sbp("wm", [P, 1], F32)
            pw = sbp("pw", [P, 1], F32)
            sc = sbp("sc", [P, 1], F32)
            s2 = sbp("s2", [P, 1], F32)
            w_in, maxed, allmax, scaled, dve, hi, first_in, first = (sem(g + n) for n in ("w_in", "maxed", "allmax", "scaled", "dve", "hi", "first_in", "first"))
            with nc.Block() as block:
                @block.sync
                def _(sp):
                    sp.dma_start(Wf[:, :, :], W.rearrange("(c p) n -> p c n", p=P)).then_inc(w_in, 16)
                    sp.dma_start(brow[:, :], bias.rearrange("(o d) -> o d", o=1).to_broadcast([P, D])).then_inc(w_in, 16)
                    for c in range(FIRST):
                        sp.dma_start(rows_of(c), own_rows(c, P)).then_inc(first_in, 16)
                    sp.wait_ge(first_in, 16 * FIRST)

                @block.gpsimd
                def _(pool):
                    pool.wait_ge(maxed, 1)
                    pool.partition_all_reduce(wm[:, :], mx[:, :], P, bass.bass_isa.ReduceOp.max).then_inc(allmax, 1)

                @block.vector
                def _(v):
                    link = Chain(v, dve)
                    v.memset(zeros[:, :], 0.0)
                    v.wait_ge(w_in, 32)
                    v.tensor_reduce(mx[:, :], Wf[:, :, :].rearrange("p c n -> p (c n)"), AX_X, ALU.max, apply_absolute_value=True).then_inc(maxed, 1)
                    link(v.tensor_reduce(bm[:, :], brow[:, :], AX_X, ALU.max, apply_absolute_value=True))
                    v.wait_ge(allmax, 1)
                    link(v.scalar_tensor_tensor(bm[:, :], wm[:, :], float(D), bm[:, :], ALU.mult, ALU.add))
                    power_scale(nc, v, link, wm[:, :], pw[:, :], sc[:, :], inv[:, :], TOP)
                    v.nop().then_inc(scaled, 1)
                    if layer == 1:
                        link(v.tensor_scalar(inv[:, :], inv[:, :], 1.0 / (XS * AS), None, ALU.mult))
                        power_scale(nc, v, link, bm[:, :], pw[:, :], s2[:, :], back[:, :], TOP)
                        link(v.tensor_scalar(dinv_s2[:, :], dinv[:, :], s2[:, 0:1], None, ALU.mult))
                    else:
                        link(v.tensor_scalar(inv[:, :], inv[:, :], 1.0 / AS, None, ALU.mult))
                        link(v.tensor_tensor(inv[:, :], inv[:, :], back[:, :], ALU.mult))
                    v.wait_ge(hi, 1)
                    v.scalar_tensor_tensor(Wl[:, :, :].rearrange("p c n -> p (c n)"), Wf[:, :, :].rearrange("p c n -> p (c n)"), sc[:, 0:1],
                                           Wh[:, :, :].rearrange("p c n -> p (c n)"), ALU.mult, ALU.subtract)

                @block.scalar
                def _(act):
                    act.wait_ge(scaled, 1)
                    nc.scalar.activation(Wh[:, :, :], Wf[:, :, :], ACT.Copy, scale=sc[:, 0:1]).then_inc(hi, 1)
                    if layer == 1:
                        act.wait_ge(first_in, 16 * FIRST)
                        for c in range(QUAD):
                            normalise(c, first)

        ring = sb("ring", [P, RING, 2, 2 * D], F16)
        pick = sb("pick", [P, QUAD, 2, P], F16)
        rows_i = sb("rows_i", [P, 2, IW, 2], I32)
        v2 = sb("v2", [P, 2, D], F16)
        vT = sb("vT", [P, 2, D], F16)
        if layer == 1:
            stage = sb("stage", [P, 2 * D], F16)
        else:
            xb = sb("xb", [P, D], F32)
            st = sb("st", [P, 2, 6], F32)
            ag = sb("ag", [P, 2], F32)
        part = ctx.enter_context(nc.psum_tensor(g + "part", [P, 2, 1024], F32))
        ps_t = ctx.enter_context(nc.psum_tensor(g + "ps_t", [P, 2, 1024], F16))
        ps_o = ctx.enter_context(nc.psum_tensor(g + "ps_o", [P, 1024], F32))
        gathered = [sem(f"{g}gathered{r}") for r in range(2 * RING)]
        rows_in = [sem(f"{g}rows{u}") for u in range(2)]
        picked, summed, added, ready, hi_ready, lo_ready, turned, hi_back, lo_back, prod, biased, tick = (sem(g + n) for n in (
            "picked", "summed", "added", "ready", "hi_ready", "lo_ready", "turned", "hi_back", "lo_back", "prod", "biased", "tick"))
        hi_out, acc_out, lo_out, stored, x_in, stat = (sem(g + n) for n in ("hi_out", "acc_out", "lo_out", "stored", "x_in", "stat"))
        bn, own_in, filled, cleared, kept = (sem(g + n) for n in ("bn", "own_in", "filled", "cleared", "kept"))

        with nc.Block() as block:
            @block.sync
            def _(sp):
                def body(i):
                    for u in range(2):
                        c = 2 * i + u
                        if exists(c - 2, NSTEP):
                            wait(sp, summed, IW * (c - 1))
                        sp.dma_start(rows_i[:, u].rearrange("p k h -> p (k h)"), idx_dram[:, bass.ds(2 * IW * c, 2 * IW)]).then_inc(rows_in[u], 16)
                rounds(sp, NSTEP // (2 * IW), body)

            @block.gpsimd
            def _(pool):
                def body(i):
                    for r in range(2 * IW):
                        k = 2 * IW * i + r
                        u, q = r // IW, r % RING
                        if r % IW == 0:
                            pool.wait_ge(rows_in[u], 16 * (i + 1))
                            pool.sem_inc(tick, 1)
                        if exists(k - RING, NSTEP):
                            pool.wait_ge(summed, k - RING + 1)
                            pool.sem_inc(tick, 1)
                        for h in range(2):
                            pool.indirect_dma_start(out=ring[:, q, h, :], out_offset=None, in_=table,
                                                    in_offset=bass.IndirectOffsetOnAxis(ap=rows_i[:, u, r % IW, h:h + 1], axis=0)).then_inc(gathered[2 * q + h], 16)
                rounds(pool, NSTEP // (2 * IW), body)

            @block.scalar
            def _(act):
                def out_rows(b):
                    act.wait_ge(biased, b + 1 + CREDIT)
                    wait(act, stored, 16 * b)
                    act.sem_inc(tick, 1)
                    f = dinv_s2[:, bass.ds(b, 1)]
                    nc.scalar.activation(stage[:, 0:D], rows_of(b), ACT.Relu, scale=f).then_inc(hi_out, 1)
                    nc.scalar.activation(rows_of(b), rows_of(b), ACT.Relu, scale=f).then_inc(acc_out, 1)

                def store(b):
                    act.wait_ge(lo_out, b + 1 + CREDIT)
                    if layer == 1:
                        act.wait_ge(hi_out, b + 1 + CREDIT)
                        act.wait_ge(acc_out, b + 1 + CREDIT)
                        act.dma_start(h_dram[bass.ds(b * P, P), :], rows_of(b)).then_inc(kept, 16)
                        act.dma_start(table2[bass.ds(b * P, P), :], stage[:, :]).then_inc(stored, 16)
                    else:
                        act.wait_ge(stat, b + 1)
                        act.dma_start(x2_dram[bass.ds(b * P, P), :], xb[:, :]).then_inc(stored, 16)

                def load_x(b):
                    if layer == 2:
                        wait(act, stored, 16 * b)
                        rows = TAIL if isinstance(b, int) and b == NBR - 1 else P
                        act.dma_start(xb[0:rows, :], x[bass.ds(b * P, rows), :]).then_inc(x_in, 16)

                def fill(b):
                    if layer == 1:
                        wait(act, kept, 16 * (b - AR + 1))
                    rows = TAIL if layer == 1 and isinstance(b, int) and b == NBR - 1 else P
                    if rows < P:
                        nc.scalar.activation(rows_of(b), zeros[:, :], ACT.Copy).then_inc(cleared, 1)
                        act.wait_ge(cleared, 1)
                    place = rows_of(b) if rows == P else acc[0:rows, b % AR, :]
                    act.dma_start(place, own_rows(b, rows)).then_inc(own_in, 16)

                def body(b):
                    if exists(b, NBR):
                        act.wait_ge(ready, b + 1)
                        act.wait_ge(turned, b + CREDIT)
                        act.sem_inc(tick, 1)
                        nc.scalar.activation(v2[:, 0, :], rows_of(b), ACT.Copy, scale=dinv_as[:, bass.ds(b, 1)]).then_inc(hi_ready, 1)
                        if exists(b + QUAD, NBR) and not (isinstance(b, int) and b + QUAD < FIRST):
                            act.wait_ge(own_in, 16 * (b + QUAD - FIRST + 1))
                        if exists(b + QUAD, NBR) and layer == 1:
                            act.sem_inc(tick, 1)
                            normalise(b + QUAD, filled)
                        else:
                            act.sem_inc(filled, 1)
                        if exists(b + QUAD + 1, NBR) and not (isinstance(b, int) and b + QUAD + 1 < FIRST):
                            fill(b + QUAD + 1)
                    if exists(b - 2, NBR):
                        store(b - 2)
                    if exists(b - 1, NBR) and layer == 1:
                        out_rows(b - 1)
                    if exists(b, NBR):
                        act.wait_ge(turned, b + 1 + CREDIT)
                        act.wait_ge(prod, b + CREDIT)
                        nc.scalar.activation(vT[:, 0, :], ps_t[:, 0, 0:D], ACT.Copy).then_inc(hi_back, 1)
                    if exists(b - 1, NBR):
                        load_x(b - 1)
                rounds(act, NBR + 2, body, head=3, tail=QUAD + 4)
                if layer == 1:
                    act.wait_ge(kept, 16 * NBR)
                if layer == 2:
                    act.dma_start(x2_dram[NBR * P:NB * P, :], xb[:, :]).then_inc(stored, 16)
                act.wait_ge(stored, 16 * (NBR + layer - 1))

            @block.vector
            def _(v):
                def choose(k, q):
                    for h in range(2):
                        one = v.tensor_scalar(pick[:, q, h, :], iota_j[:, :], dloc[:, h, bass.ds(k, 1)], None, ALU.is_equal)
                    one.then_inc(picked, 1)

                def quad(m):
                    w = v.value_load(blk[0:1, bass.ds(m, 1)])
                    for q in range(QUAD):
                        k = QUAD * m + q
                        v.wait_ge(summed, k + 1)
                        v.wait_ge(added, k + 2)
                        rows = rows_of(w >> (6 * q))
                        v.tensor_tensor(rows, rows, part[:, q % 2, 0:D], ALU.add).then_inc(added, 1)
                        choose(k + QUAD, q)

                def finish(b):
                    v.wait_ge(prod, b + CREDIT)
                    v.scalar_tensor_tensor(rows_of(b - 1), ps_o[:, 0:D], inv[:, 0:1], brow[:, :], ALU.mult, ALU.add).then_inc(biased, 1)

                def hand_on(c):
                    if layer == 1:
                        v.wait_ge(hi_out, c + 1 + CREDIT)
                        v.wait_ge(acc_out, c + 1 + CREDIT)
                        v.tensor_tensor(stage[:, D:2 * D], rows_of(c), stage[:, 0:D], ALU.subtract).then_inc(lo_out, 1)
                    else:
                        v.wait_ge(biased, c + 1 + CREDIT)
                        v.wait_ge(x_in, 16 * (c + 1 + CREDIT))
                        v.tensor_tensor(xb[:, :], rows_of(c), xb[:, :], ALU.add).then_inc(lo_out, 1)
                        v.wait_ge(lo_out, c + 1 + CREDIT)
                        v.sem_inc(tick, 1)
                        for q in range(2):
                            v.bn_stats(st[:, q, :], xb[:, q * (D // 2):(q + 1) * (D // 2)]).then_inc(bn, 1)
                        v.wait_ge(bn, 3 * c + 2 + 4 * CREDIT)
                        v.sem_inc(stat, 1)
                        v.bn_aggr(ag[:, :], st[:, :, :].rearrange("p q s -> p (q s)")).then_inc(bn, 1)
                        v.wait_ge(bn, 3 * c + 3 + 4 * CREDIT)
                        v.sem_inc(tick, 1)
                        at = c if isinstance(c, int) else c.with_bounds(min_val=0, max_val=NBR - 1)
                        v.tensor_copy(mv2[:, bass.ds(at, 1), :].rearrange("p o d -> p (o d)"), ag[:, :])

                def visit(b, m):
                    v.wait_ge(added, QUAD * m + 2)
                    v.sem_inc(ready, 1)
                    v.wait_ge(hi_ready, b + 1)
                    v.wait_ge(turned, b + CREDIT)
                    v.scalar_tensor_tensor(v2[:, 1, :], rows_of(b), dinv_as[:, bass.ds(b, 1)], v2[:, 0, :],
                                           ALU.mult, ALU.subtract).then_inc(lo_ready, 1)
                    with v.If(b > 1):
                        hand_on(b - 2)
                    with v.If(b > 0):
                        finish(b)
                    v.wait_ge(turned, b + 1 + CREDIT)
                    v.wait_ge(prod, b + CREDIT)
                    v.wait_ge(filled, b + 1)
                    v.tensor_copy(vT[:, 1, :], ps_t[:, 1, 0:D]).then_inc(lo_back, 1)

                v.sem_inc(added, 2)
                for count, n in ((turned, 1), (prod, 1), (biased, 1), (lo_out, 1)) + (((hi_out, 1), (acc_out, 1)) if layer == 1 else ((x_in, 16), (bn, 4))):
                    v.sem_inc(count, n * CREDIT)
                for q in range(QUAD):
                    choose(q, q)
                all_events(v, ev, quad, visit)
                hand_on(NBR - 2)
                finish(NBR)
                hand_on(NBR - 1)

            @block.tensor
            def _(pe):
                def steps(m, odd):
                    for q in range(QUAD):
                        k = QUAD * m + q
                        at = QUAD * odd + q
                        pe.wait_ge(picked, k + 1)
                        pe.wait_ge(added, k + 1)
                        for h in range(2):
                            pe.wait_ge(gathered[2 * at + h], 16 * ((m >> 1) + 1))
                            for half in range(2):
                                for a, z in ((0, 512), (512, D)):
                                    mm = nc.tensor.matmul(part[:, q % 2, a:z], pick[:, q, h, :], ring[:, at, h, half * D + a:half * D + z],
                                                          start=(h == 0 and half == 0), stop=(h == 1 and half == 1))
                        mm.then_inc(summed, 1)

                def quad(m):
                    with pe.If((m & 1) > 0):
                        steps(m, 1)
                    with pe.Else():
                        steps(m, 0)

                def multiply(b):
                    pe.wait_ge(hi_back, b)
                    pe.wait_ge(lo_back, b)
                    for c in range(DC):
                        for half, Ws in ((0, (Wh, Wl)), (1, (Wh,))):
                            for Wp in Ws:
                                for a, z in ((0, 512), (512, D)):
                                    mm = nc.tensor.matmul(ps_o[:, a:z], vT[:, half, c * P:(c + 1) * P], Wp[:, c, a:z],
                                                          start=(c == 0 and half == 0 and Wp is Wh), stop=(c == DC - 1 and half == 1))
                    mm.then_inc(prod, 1)

                def visit(b, m):
                    with pe.If(b > 0):
                        multiply(b)
                    pe.wait_ge(hi_ready, b + 1)
                    pe.wait_ge(lo_ready, b + 1)
                    for half in range(2):
                        for c in range(DC):
                            mm = nc.tensor.transpose(ps_t[:, half, c * P:(c + 1) * P], v2[:, half, c * P:(c + 1) * P], ident16[:, :])
                    mm.then_inc(turned, 1)
                all_events(pe, ev, quad, visit)
                multiply(NBR)


def dispatch(nc, phi, scale, x2_dram, cw_dram, slots, mv, valid, ident16):
    with ExitStack() as ctx:
        sems = phase_semaphores(nc, ctx)

        def sem(name):
            sems.append(nc.alloc_semaphore(name))
            return sems[-1]

        def sb(name, shape, dt):
            return ctx.enter_context(nc.sbuf_tensor("s_" + name, shape, dt))

        phi_h = sb("phi_h", [P, DC, K], F16)
        phi_l = sb("phi_l", [P, DC, K], F16)
        scl = sb("scl", [P, 1], F32)
        xf = sb("xf", [P, NB], F32)
        xc = sb("xc", [P, NB], F32)
        with ExitStack() as pre:
            def sbp(name, shape, dt):
                return pre.enter_context(nc.sbuf_tensor("s_" + name, shape, dt))
            phi_f = sbp("phi_f", [P, DC, K], F32)
            sq = sbp("sq", [P, DC, K], F32)
            norm = sbp("norm", [P, K], F32)
            ones32 = sbp("ones32", [P, P], F32)
            var = sbp("var", [P, 2, NB], F32)
            ps_n = pre.enter_context(nc.psum_tensor("s_ps_n", [P, 1024], F32))
            p_in, squared, normed, rooted, unit, hi, ones, var_r, std_r, dve = (
                sem("p_" + n) for n in ("p_in", "squared", "normed", "rooted", "unit", "hi", "ones", "var_r", "std_r", "dve"))
            with nc.Block() as block:
                @block.sync
                def _(sp):
                    sp.dma_start(phi_f[:, :, :], phi.rearrange("(c p) e s -> p c (e s)", p=P)).then_inc(p_in, 16)
                    sp.dma_start(scl[:, :], scale.rearrange("(o d) -> o d", o=1).to_broadcast([P, 1])).then_inc(p_in, 16)

                @block.tensor
                def _(pe):
                    pe.wait_ge(ones, 1)
                    pe.wait_ge(squared, 1)
                    for a in (0, 512):
                        for c in range(DC):
                            mm = nc.tensor.matmul(ps_n[:, a:a + 512], ones32[:, :], sq[:, c, a:a + 512], start=(c == 0), stop=(c == DC - 1))
                    mm.then_inc(normed, 1)

                @block.scalar
                def _(act):
                    act.wait_ge(var_r, 2)
                    nc.scalar.activation(var[:, :, :], var[:, :, :], ACT.Sqrt).then_inc(std_r, 1)
                    act.wait_ge(normed, 1)
                    nc.scalar.activation(norm[:, :], ps_n[:, :], ACT.Sqrt).then_inc(rooted, 1)
                    act.wait_ge(unit, 1)
                    nc.scalar.activation(phi_h[:, :, :], phi_f[:, :, :], ACT.Copy, scale=US).then_inc(hi, 1)

                @block.vector
                def _(v):
                    link = Chain(v, dve)
                    v.memset(ones32[:, :], 1.0).then_inc(ones, 1)
                    v.tensor_scalar(var[:, 0, :], mv[:, :, 1], EPS_LN, None, ALU.add).then_inc(var_r, 1)
                    v.tensor_scalar(var[:, 1, :], mv[:, :, 1], float(D), None, ALU.mult).then_inc(var_r, 1)
                    v.wait_ge(p_in, 32)
                    v.tensor_tensor(sq[:, :, :], phi_f[:, :, :], phi_f[:, :, :], ALU.mult).then_inc(squared, 1)
                    link(v.tensor_scalar(scl[:, :], scl[:, :], 1.0 / (US * US), None, ALU.mult))
                    v.wait_ge(std_r, 1)
                    link(v.reciprocal(var[:, 0, :], var[:, 0, :]))
                    link(v.tensor_tensor(var[:, 1, :], var[:, 1, :], var[:, 0, :], ALU.mult))
                    link(v.tensor_scalar(var[:, 1, :], var[:, 1, :], EPS_L2, None, ALU.max))
                    link(v.reciprocal(var[:, 1, :], var[:, 1, :]))
                    link(v.scalar_tensor_tensor(xf[:, :], var[:, 0, :], US, var[:, 1, :], ALU.mult, ALU.mult))
                    link(v.tensor_tensor(xf[:, :], xf[:, :], valid[:, :], ALU.mult))
                    link(v.scalar_tensor_tensor(xc[:, :], mv[:, :, 0], -1.0, xf[:, :], ALU.mult, ALU.mult))
                    v.wait_ge(rooted, 1)
                    link(v.tensor_scalar(norm[:, :], norm[:, :], EPS_L2, None, ALU.max))
                    link(v.reciprocal(norm[:, :], norm[:, :]))
                    v.tensor_tensor(phi_f[:, :, :], phi_f[:, :, :], norm[:, :].unsqueeze(1).to_broadcast([P, DC, K]), ALU.mult).then_inc(unit, 1)
                    v.wait_ge(unit, 1)
                    v.wait_ge(hi, 1)
                    v.scalar_tensor_tensor(phi_l[:, :, :].rearrange("p c n -> p (c n)"), phi_f[:, :, :].rearrange("p c n -> p (c n)"), US,
                                           phi_h[:, :, :].rearrange("p c n -> p (c n)"), ALU.mult, ALU.subtract)

        RB = 4 * GB
        HR = RB // 2
        xin = sb("xin", [P, 2, D], F32)
        xn = sb("xn", [P, RB, 2, D], F16)
        xT = sb("xT", [P, 2, 2, D], F16)
        lg = sb("lg", [P, 2, K], F32)
        dwf = sb("dwf", [P, 2, K], F32)
        cwf = sb("cwf", [P, 2, K], F32)
        dw = sb("dw", [P, RB, 2, K], F16)
        cst = sb("cst", [P, 2, 2 * K], F16)
        m = sb("m", [P, 2, NX], F32)
        nM = sb("nM", [P, 2], F32)
        em = sb("em", [P, 2, NX], F32)
        z = sb("z", [P, 2, NX], F32)
        rz = sb("rz", [P, 2, NX], F32)
        wz = sb("wz", [P, 2, NX], F32)
        Z = sb("Z", [P, 2], F32)
        g = sb("g", [P, 2, NX], F32)
        ps_t = ctx.enter_context(nc.psum_tensor("s_pt", [P, 2, 1024], F16))
        ps_l = ctx.enter_context(nc.psum_tensor("s_pl", [P, 2, 1024], F32))
        ps_s = ctx.enter_context(nc.psum_tensor("s_ps", [P, 2, 512], F32))
        (xn_hi, xn_f, xn_lo, turned, hi_back, lo_back, logits, scaled, maxed, shifted, em_r, expd, dwf_r, g_r, dw_hi,
         dw_lo, cwf_r, cw_hi, cw_lo, tiles, added, dve, tick) = (sem("m_" + n) for n in (
             "xn_hi", "xn_f", "xn_lo", "turned", "hi_back", "lo_back", "logits", "scaled", "maxed", "shifted", "em_r", "expd",
             "dwf_r", "g_r", "dw_hi", "dw_lo", "cwf_r", "cw_hi", "cw_lo", "tiles", "added", "dve", "tick"))
        x_in = [sem("m_x0"), sem("m_x1")]
        stored = [sem("m_st0"), sem("m_st1")]
        NT = 2 * DC
        LINKS = 7
        n = (NB + GB + 4 + RB - 1) // RB

        def by_expert(ap):
            return ap.rearrange("p (e s) -> p e s", s=NS)

        def group_of(j, s):
            gr = HR * j + (s - 5) // GB
            return (gr, NT // GB * ((s - 5) % GB)) if exists(gr, NB // GB) else (None, 0)

        with nc.Block() as block:
            @block.sync
            def _(sp):
                def body(j):
                    for s in range(RB):
                        i = RB * j + s
                        if exists(i, NB):
                            wait(sp, xn_lo, i - 1)
                            sp.dma_start(xin[:, s % 2, :], x2_dram[bass.ds(i * P, P), :]).then_inc(x_in[s % 2], 16)
                        b = i - 4
                        if exists(b, NB):
                            sp.wait_ge(cw_hi, b + 1)
                            sp.wait_ge(cw_lo, b + 1)
                            sp.dma_start(cw_dram[bass.ds(b * P, P), :], cst[:, s % 2, :]).then_inc(stored[s % 2], 16)
                rounds(sp, n, body)
                for s in range(2):
                    sp.wait_ge(stored[s], 16 * (NB // 2))

            @block.scalar
            def _(act):
                def body(j):
                    for s in range(RB):
                        i = RB * j + s
                        t = s % 2
                        if exists(i, NB):
                            act.wait_ge(x_in[t], 16 * (HR * j + s // 2 + 1))
                            wait(act, tiles, NT * (HR * j + s // GB - RB // GB + 1))
                            act.sem_inc(tick, 1)
                            f, c = xf[:, bass.ds(i, 1)], xc[:, bass.ds(i, 1)]
                            nc.scalar.activation(xn[:, s, 0, :], xin[:, t, :], ACT.Identity, bias=c, scale=f).then_inc(xn_hi, 1)
                            nc.scalar.activation(xin[:, t, :], xin[:, t, :], ACT.Identity, bias=c, scale=f).then_inc(xn_f, 1)
                        if exists(i - 1, NB):
                            act.wait_ge(turned, i)
                            wait(act, logits, i - 2)
                            nc.scalar.activation(xT[:, 1 - t, 0, :], ps_t[:, 0, 0:D], ACT.Copy).then_inc(hi_back, 1)
                        b, u = i - 3, 1 - t
                        if exists(b, NB):
                            act.wait_ge(logits, b + 1)
                            wait(act, dwf_r, b - 1)
                            nc.scalar.activation(lg[:, u, :], ps_l[:, u, :], ACT.Copy, scale=scl[:, 0:1]).then_inc(scaled, 1)
                            act.wait_ge(maxed, b + 1)
                            wait(act, g_r, b - 1)
                            nc.scalar.activation(em[:, u, :], m[:, u, :], ACT.Exp, bias=nM[:, u:u + 1]).then_inc(em_r, 1)
                            act.wait_ge(shifted, b + 1)
                            nc.scalar.activation(lg[:, u, :], lg[:, u, :], ACT.Exp).then_inc(expd, 1)
                            act.wait_ge(dwf_r, b + 1)
                            nc.scalar.activation(dw[:, (s - 3) % RB, 0, :], dwf[:, u, :], ACT.Copy).then_inc(dw_hi, 1)
                            act.wait_ge(cwf_r, b + 1)
                            wait(act, stored[u], 16 * (HR * j + (s - 3) // 2))
                            nc.scalar.activation(cst[:, u, 0:K], cwf[:, u, :], ACT.Copy).then_inc(cw_hi, 1)
                rounds(act, n, body)

            @block.vector
            def _(v):
                link = Chain(v, dve)

                def add(gr, u):
                    tile = NT * gr + u
                    v.wait_ge(tiles, tile + 1)
                    c, a = u // 2, 512 * (u % 2)
                    dst_s = slots[:, c, a:a + 512]
                    if isinstance(gr, int) and gr == 0:
                        v.tensor_copy(dst_s, ps_s[:, u % 2, :]).then_inc(added, 1)
                    else:
                        wait(v, added, tile - NT + 1)
                        v.tensor_tensor(dst_s, dst_s, ps_s[:, u % 2, :], ALU.add).then_inc(added, 1)

                def body(j):
                    for s in range(RB):
                        i = RB * j + s
                        t = s % 2
                        gr, u0 = group_of(j, s)

                        def sums(first, last):
                            if gr is not None:
                                for u in range(first, last):
                                    add(gr, u0 + u)
                        if exists(i - 1, NB):
                            v.wait_ge(turned, i)
                            wait(v, logits, i - 2)
                            v.tensor_copy(xT[:, 1 - t, 1, :], ps_t[:, 1, 0:D]).then_inc(lo_back, 1)
                        if exists(i, NB):
                            v.wait_ge(xn_hi, i + 1)
                            v.wait_ge(xn_f, i + 1)
                            v.tensor_tensor(xn[:, s, 1, :], xin[:, t, :], xn[:, s, 0, :], ALU.subtract).then_inc(xn_lo, 1)
                        b, t = i - 3, 1 - t
                        if exists(b, NB):
                            link.at(LINKS * b)
                            v.wait_ge(scaled, b + 1)
                            wait(v, em_r, b - 1)
                            link(v.tensor_reduce(m[:, t, :], by_expert(lg[:, t, :]), AX_X, ALU.max))
                            v.tensor_reduce(nM[:, t:t + 1], m[:, t, :], AX_X, ALU.max, negate=True).then_inc(maxed, 1)
                            v.tensor_tensor(by_expert(lg[:, t, :]), by_expert(lg[:, t, :]), m[:, t, :].unsqueeze(2).to_broadcast([P, NX, NS]),
                                            ALU.subtract).then_inc(shifted, 1)
                        sums(0, 2)
                        if exists(b, NB):
                            v.wait_ge(expd, b + 1)
                            link(v.tensor_reduce(z[:, t, :], by_expert(lg[:, t, :]), AX_X, ALU.add))
                            link(v.reciprocal(rz[:, t, :], z[:, t, :]))
                            link(v.tensor_scalar(rz[:, t, :], rz[:, t, :], PS, None, ALU.mult))
                            wait(v, cwf_r, b - 1)
                            v.tensor_tensor(by_expert(dwf[:, t, :]), by_expert(lg[:, t, :]), rz[:, t, :].unsqueeze(2).to_broadcast([P, NX, NS]),
                                            ALU.mult).then_inc(dwf_r, 1)
                        sums(2, 3)
                        if exists(b, NB):
                            v.wait_ge(em_r, b + 1)
                            link(v.tensor_tensor(wz[:, t, :], z[:, t, :], em[:, t, :], ALU.mult))
                            link(v.tensor_reduce(Z[:, t:t + 1], wz[:, t, :], AX_X, ALU.add))
                            link(v.reciprocal(Z[:, t:t + 1], Z[:, t:t + 1]))
                            v.tensor_scalar(g[:, t, :], wz[:, t, :], Z[:, t:t + 1], None, ALU.mult).then_inc(g_r, 1)
                            v.wait_ge(dwf_r, b + 1)
                            v.wait_ge(dw_hi, b + 1)
                            v.tensor_tensor(dw[:, (s - 3) % RB, 1, :], dwf[:, t, :], dw[:, (s - 3) % RB, 0, :], ALU.subtract).then_inc(dw_lo, 1)
                            assert link.n == LINKS
                        sums(3, 6)
                rounds(v, n, body)

            @block.gpsimd
            def _(pool):
                def body(j):
                    for s in range(RB):
                        b = RB * j + s - 3
                        t = 1 - s % 2
                        if exists(b, NB):
                            pool.wait_ge(g_r, b + 1)
                            pool.wait_ge(dwf_r, b + 1)
                            wait(pool, cw_hi, b - 1)
                            pool.tensor_tensor(by_expert(cwf[:, t, :]), by_expert(dwf[:, t, :]), g[:, t, :].unsqueeze(2).to_broadcast([P, NX, NS]),
                                               ALU.mult).then_inc(cwf_r, 1)
                            pool.wait_ge(cwf_r, b + 1)
                            pool.wait_ge(cw_hi, b + 1)
                            wait(pool, stored[t], 16 * (HR * j + (s - 3) // 2))
                            pool.tensor_tensor(cst[:, t, K:2 * K], cwf[:, t, :], cst[:, t, 0:K], ALU.subtract).then_inc(cw_lo, 1)
                rounds(pool, n, body)

            @block.tensor
            def _(pe):
                def body(j):
                    for s in range(RB):
                        i = RB * j + s
                        t = s % 2
                        if exists(i - 1, NB):
                            pe.wait_ge(xn_lo, i)
                            wait(pe, hi_back, i - 1)
                            wait(pe, lo_back, i - 1)
                            for half in range(2):
                                for c in range(DC):
                                    mm = nc.tensor.transpose(ps_t[:, half, c * P:(c + 1) * P], xn[:, (s - 1) % RB, half, c * P:(c + 1) * P], ident16[:, :])
                            mm.then_inc(turned, 1)
                        b = i - 2
                        gr, u0 = group_of(j, s)
                        if exists(b, NB):
                            pe.wait_ge(hi_back, b + 1)
                            pe.wait_ge(lo_back, b + 1)
                            wait(pe, scaled, b - 1)
                        for c in range(DC):
                            if exists(b, NB):
                                for half, ph in ((0, phi_h), (0, phi_l), (1, phi_h)):
                                    for a in (0, 512):
                                        mm = nc.tensor.matmul(ps_l[:, t, a:a + 512], xT[:, t, half, c * P:(c + 1) * P], ph[:, c, a:a + 512],
                                                              start=(c == 0 and half == 0 and ph is phi_h), stop=(c == DC - 1 and half == 1))
                                if c == DC - 1:
                                    mm.then_inc(logits, 1)
                            if gr is not None:
                                first = (s - 5) // GB * GB % RB
                                u = u0 + c
                                k, a = u // 2, 512 * (u % 2)
                                pe.wait_ge(dw_lo, GB * (gr + 1))
                                wait(pe, added, NT * gr + u - 1)
                                for q in range(first, first + GB):
                                    for xh, dh in ((0, 0), (0, 1), (1, 0)):
                                        mm = nc.tensor.matmul(ps_s[:, u % 2, :], xn[:, q, xh, k * P:(k + 1) * P], dw[:, q, dh, a:a + 512],
                                                              start=(q == first and xh == 0 and dh == 0), stop=(q == first + GB - 1 and xh == 1))
                                mm.then_inc(tiles, 1)
                rounds(pe, n, body)


def experts(nc, w1, eb1, w2, eb2, slots, eo, ident16):
    with ExitStack() as ctx:
        sems = phase_semaphores(nc, ctx)

        def sem(name):
            sems.append(nc.alloc_semaphore(name))
            return sems[-1]

        def sb(name, shape, dt):
            return ctx.enter_context(nc.sbuf_tensor("e_" + name, shape, dt))

        G = P // NS
        NG = NX // G
        w1s = sb("w1s", [P, 2 * G, DC, H], F32)
        w2s = sb("w2s", [P, G, HC, D], F32)
        bias1 = sb("bias1", [P, 2, H], F32)
        bias2 = sb("bias2", [P, 2, D], F32)
        ident32 = sb("ident32", [P, P], F32)
        sl = sb("sl", [P, 2, DC, P], F32)
        hb = sb("hb", [P, 2, H], F32)
        hT = sb("hT", [P, H], F32)
        ps_h = ctx.enter_context(nc.psum_tensor("e_ph", [P, 2, 512], F32))
        ps_g = ctx.enter_context(nc.psum_tensor("e_pg", [P, 512], F32))
        ps_e = ctx.enter_context(nc.psum_tensor("e_pe", [P, 2, 1024], F32))
        w1_in = [sem(f"w1_in{q}") for q in range(2 * G)]
        w2_in = [sem(f"w2_in{q}") for q in range(G)]
        b1_in = [sem(f"b1_in{q}") for q in range(2)]
        b2_in = [sem(f"b2_in{q}") for q in range(2)]
        sl_r, up, hb_r, act_r, turned, back, down, eo_r, tick = (sem("e_" + n) for n in (
            "sl_r", "up", "hb_r", "act_r", "turned", "back", "down", "eo_r", "tick"))
        ident_r = sem("e_ident")
        n = NG // 2 + 1
        eb1_v = eb1.rearrange("(g j) (o h) -> g j o h", j=G, o=1)
        eb2_v = eb2.rearrange("(g j) (o h) -> g j o h", j=G, o=1)
        w1_v = w1.rearrange("e (c p) h -> p e c h", p=P)
        w2_v = w2.rearrange("e (c p) d -> p e c d", p=P)

        with nc.Block() as block:
            @block.sync
            def _(sp):
                def load_up(i, s):
                    wait(sp, up, i - 1)
                    for q in range(G):
                        sp.dma_start(w1s[:, G * s + q], w1_v[:, bass.ds(i * G + q, 1), :, :].rearrange("p o c h -> p (o c) h")).then_inc(w1_in[G * s + q], 16)

                def body(j):
                    for s in range(2):
                        i = 2 * j + s
                        if exists(i, NG):
                            wait(sp, hb_r, i - 1)
                            for q in range(G):
                                sp.dma_start(bias1[NS * q:NS * (q + 1), s, :], eb1[bass.ds(i * G + q, 1), :].to_broadcast([NS, H])).then_inc(b1_in[s], 16)
                            wait(sp, eo_r, i - 1)
                            for q in range(G):
                                sp.dma_start(bias2[NS * q:NS * (q + 1), s, :], eb2[bass.ds(i * G + q, 1), :].to_broadcast([NS, D])).then_inc(b2_in[s], 16)
                            if isinstance(i, int) and i == 0:
                                load_up(0, 0)
                            if exists(i + 1, NG):
                                load_up(i + 1, 1 - s)
                            wait(sp, down, i)
                            for q in range(G):
                                sp.dma_start(w2s[:, q], w2_v[:, bass.ds(i * G + q, 1), :, :].rearrange("p o c h -> p (o c) h")).then_inc(w2_in[q], 16)
                rounds(sp, n, body, head=2, tail=2)

            @block.scalar
            def _(act):
                def body(j):
                    for s in range(2):
                        i = 2 * j + s
                        if exists(i, NG):
                            wait(act, up, i - 1)
                            act.sem_inc(tick, 1)
                            nc.scalar.activation(sl[:, s], slots[:, :, bass.ds(i * P, P)], ACT.Copy, scale=1.0 / (US * PS)).then_inc(sl_r, 1)
                        if exists(i, NG):
                            act.wait_ge(hb_r, i + 1)
                            nc.scalar.activation(hb[:, s, :], hb[:, s, :], ACT.Gelu).then_inc(act_r, 1)
                        if exists(i - 1, NG):
                            act.wait_ge(turned, i)
                            wait(act, down, i - 1)
                            nc.scalar.activation(hT[:, :], ps_g[:, 0:H], ACT.Copy).then_inc(back, 1)
                rounds(act, n, body, head=2)

            @block.vector
            def _(v):
                v.tensor_copy(ident32[:, :], ident16[:, :]).then_inc(ident_r, 1)

                def body(j):
                    for s in range(2):
                        i = 2 * j + s
                        if exists(i, NG):
                            v.wait_ge(up, i + 1)
                            v.wait_ge(b1_in[s], 16 * G * (j + 1))
                            wait(v, turned, i - 1)
                            v.tensor_tensor(hb[:, s, :], ps_h[:, s, 0:H], bias1[:, s, :], ALU.add).then_inc(hb_r, 1)
                        if exists(i - 1, NG):
                            v.wait_ge(down, i)
                            v.wait_ge(b2_in[1 - s], 16 * G * (j + s))
                            v.tensor_tensor(eo[:, bass.ds(i - 1, 1), :].rearrange("p o d -> p (o d)"), ps_e[:, 1 - s, 0:D], bias2[:, 1 - s, :],
                                            ALU.add).then_inc(eo_r, 1)
                rounds(v, n, body, head=2)

            @block.tensor
            def _(pe):
                def body(j):
                    for s in range(2):
                        i = 2 * j + s
                        if exists(i, NG):
                            pe.wait_ge(sl_r, i + 1)
                            wait(pe, hb_r, i - 1)
                            for q in range(G):
                                pe.wait_ge(w1_in[G * s + q], 16 * (j + 1))
                            for c in range(DC):
                                for q in range(G):
                                    mm = nc.tensor.matmul(ps_h[NS * q:NS * (q + 1), s, 0:H], sl[:, s, c, NS * q:NS * (q + 1)], w1s[:, G * s + q, c, :],
                                                          start=(c == 0), stop=(c == DC - 1))
                            mm.then_inc(up, 1)
                        if exists(i - 1, NG):
                            pe.wait_ge(ident_r, 1)
                            pe.wait_ge(act_r, i)
                            wait(pe, back, i - 1)
                            for c in range(HC):
                                mm = nc.tensor.transpose(ps_g[:, c * P:(c + 1) * P], hb[:, 1 - s, c * P:(c + 1) * P], ident32[:, :])
                            mm.then_inc(turned, 1)
                            pe.wait_ge(back, i)
                            wait(pe, eo_r, i - 2)
                            for q in range(G):
                                pe.wait_ge(w2_in[q], 16 * i)
                            for c in range(HC):
                                for a, e in ((0, 512), (512, D)):
                                    for q in range(G):
                                        mm = nc.tensor.matmul(ps_e[NS * q:NS * (q + 1), 1 - s, a:e], hT[:, c * P + NS * q:c * P + NS * (q + 1)], w2s[:, q, c, a:e],
                                                              start=(c == 0), stop=(c == HC - 1))
                            mm.then_inc(down, 1)
                rounds(pe, n, body, head=2)


def combine(nc, eo, cw_dram, x2_dram, ident16, out):
    with ExitStack() as ctx:
        sems = phase_semaphores(nc, ctx)

        def sem(name):
            sems.append(nc.alloc_semaphore(name))
            return sems[-1]

        def sb(name, shape, dt):
            return ctx.enter_context(nc.sbuf_tensor("c_" + name, shape, dt))

        eh = sb("eh", [P, KC, D], F16)
        el = sb("el", [P, KC, D], F16)
        inv = sb("inv", [P, 1], F32)
        mx = sb("mx", [P, 1], F32)
        am = sb("am", [P, 1], F32)
        pw = sb("pw", [P, 1], F32)
        sc = sb("sc", [P, 1], F32)
        cw = sb("cw", [P, 2, 2 * K], F16)
        cT = sb("cT", [P, 2, 2, K], F16)
        xb = sb("xb", [P, 2, D], F32)
        ob = sb("ob", [P, 2, D], F32)
        ps_t = ctx.enter_context(nc.psum_tensor("c_pt", [P, 2, 2, 1024], F16))
        ps_o = ctx.enter_context(nc.psum_tensor("c_po", [P, 2, 1024], F32))
        maxed, allmax, scaled, e_hi, e_lo, dve, turned, hi_back, lo_back, prod, summed = (sem("c_" + n) for n in (
            "maxed", "allmax", "scaled", "e_hi", "e_lo", "dve", "turned", "hi_back", "lo_back", "prod", "summed"))
        cw_in = [sem("c_cw0"), sem("c_cw1")]
        x_in = [sem("c_x0"), sem("c_x1")]
        stored = [sem("c_st0"), sem("c_st1")]
        n = (NBR + 1) // 2
        with nc.Block() as block:
            @block.sync
            def _(sp):
                def body(j):
                    for s in range(2):
                        i = 2 * j + s
                        if exists(i, NBR):
                            wait(sp, turned, i - 1)
                            sp.dma_start(cw[:, s, :], cw_dram[bass.ds(i * P, P), :]).then_inc(cw_in[s], 16)
                            wait(sp, summed, i - 1)
                            sp.dma_start(xb[:, s, :], x2_dram[bass.ds(i * P, P), :]).then_inc(x_in[s], 16)
                        b = i - 2
                        if exists(b, NBR):
                            sp.wait_ge(summed, b + 1)
                            rows = TAIL if isinstance(b, int) and b == NBR - 1 else P
                            sp.dma_start(out[bass.ds(b * P, rows), :], ob[0:rows, s, :]).then_inc(stored[s], 16)
                rounds(sp, n + 1, body, head=2, tail=2)
                sp.wait_ge(stored[0], 16 * n)
                sp.wait_ge(stored[1], 16 * (NBR - n))

            @block.gpsimd
            def _(pool):
                pool.wait_ge(maxed, 1)
                pool.partition_all_reduce(am[:, :], mx[:, :], P, bass.bass_isa.ReduceOp.max).then_inc(allmax, 1)

            @block.scalar
            def _(act):
                act.wait_ge(scaled, 1)
                nc.scalar.activation(eh[:, :, :], eo[:, :, :], ACT.Copy, scale=sc[:, 0:1]).then_inc(e_hi, 1)

                def body(j):
                    for s in range(2):
                        i = 2 * j + s
                        if exists(i, NBR):
                            act.wait_ge(turned, i + 1)
                            wait(act, prod, i - 1)
                            nc.scalar.activation(cT[:, s, 0, :], ps_t[:, s, 0, :], ACT.Copy).then_inc(hi_back, 1)
                rounds(act, n, body, head=2)

            @block.vector
            def _(v):
                link = Chain(v, dve)
                v.tensor_reduce(mx[:, :], eo[:, :, :].rearrange("p c d -> p (c d)"), AX_X, ALU.max, apply_absolute_value=True).then_inc(maxed, 1)
                v.wait_ge(allmax, 1)
                power_scale(nc, v, link, am[:, :], pw[:, :], sc[:, :], inv[:, :], TOP)
                v.nop().then_inc(scaled, 1)
                link(v.tensor_scalar(inv[:, :], inv[:, :], 1.0 / PS, None, ALU.mult))
                v.wait_ge(e_hi, 1)
                v.scalar_tensor_tensor(el[:, :, :].rearrange("p c d -> p (c d)"), eo[:, :, :].rearrange("p c d -> p (c d)"), sc[:, 0:1],
                                       eh[:, :, :].rearrange("p c d -> p (c d)"), ALU.mult, ALU.subtract).then_inc(e_lo, 1)

                def body(j):
                    for s in range(2):
                        i = 2 * j + s
                        if exists(i, NBR):
                            v.wait_ge(turned, i + 1)
                            wait(v, prod, i - 1)
                            v.tensor_copy(cT[:, s, 1, :], ps_t[:, s, 1, :]).then_inc(lo_back, 1)
                        b = i - 1
                        if exists(b, NBR):
                            v.wait_ge(prod, b + 1)
                            v.wait_ge(x_in[1 - s], 16 * (j + s))
                            wait(v, stored[1 - s], 16 * (j + s - 1))
                            v.scalar_tensor_tensor(ob[:, 1 - s, :], ps_o[:, 1 - s, 0:D], inv[:, 0:1], xb[:, 1 - s, :], ALU.mult, ALU.add).then_inc(summed, 1)
                rounds(v, n, body, head=2)

            @block.tensor
            def _(pe):
                def body(j):
                    for s in range(2):
                        i = 2 * j + s
                        if exists(i, NBR):
                            pe.wait_ge(cw_in[s], 16 * (j + 1))
                            wait(pe, hi_back, i - 1)
                            wait(pe, lo_back, i - 1)
                            for half in range(2):
                                for c in range(KC):
                                    mm = nc.tensor.transpose(ps_t[:, s, half, c * P:(c + 1) * P], cw[:, s, half * K + c * P:half * K + (c + 1) * P], ident16[:, :])
                            mm.then_inc(turned, 1)
                        b = i - 1
                        if exists(b, NBR):
                            pe.wait_ge(hi_back, b + 1)
                            pe.wait_ge(lo_back, b + 1)
                            pe.wait_ge(e_lo, 1)
                            wait(pe, summed, b - 1)
                            for c in range(KC):
                                for half, ee in ((0, eh), (0, el), (1, eh)):
                                    for a, e in ((0, 512), (512, D)):
                                        mm = nc.tensor.matmul(ps_o[:, 1 - s, a:e], cT[:, 1 - s, half, c * P:(c + 1) * P], ee[:, c, a:e],
                                                              start=(c == 0 and half == 0 and ee is eh), stop=(c == KC - 1 and half == 1))
                            mm.then_inc(prod, 1)
                rounds(pe, n, body, head=2)


_INS = ["x", "src", "dst", "L0_gnn_W1", "L0_gnn_b1", "L0_gnn_W2", "L0_gnn_b2", "L0_ffn_phi", "L0_ffn_scale",
        "L0_ffn_w1", "L0_ffn_b1", "L0_ffn_w2", "L0_ffn_b2"]


def kernel(**inputs):
    import numpy as _np
    import concourse.bacc as _bacc
    from concourse import mybir as _mybir
    from concourse.bass_utils import run_bass_kernel_spmd as _run

    nc = _bacc.Bacc("TRN2", target_bir_lowering=False, num_devices=1)
    arrays, args = {}, []
    for name in _INS:
        a = _np.ascontiguousarray(inputs[name])
        arrays[f"in_{name}_dram"] = a
        args.append(nc.dram_tensor(f"in_{name}_dram", a.shape, _mybir.dt.from_np(a.dtype), kind="ExternalInput").ap())
    out = nc.dram_tensor("out_0_dram", (N, D), F32, kind="ExternalOutput").ap()
    gnn_ffn(nc, *args, out)
    r = _run(nc, [arrays], core_ids=[0])
    return r.results[0]["out_0_dram"]
```
